# Optimizing a Trainium2 kernel written in Bass

```python
import numpy as np
import jax
import jax.numpy as jnp

def _softmax(x, axis=-1):
    return jax.nn.softmax(x, axis=axis)

def _gelu(x):
    return jax.nn.gelu(x, approximate=True)

def _silu(x):
    return jax.nn.silu(x)

def _sigmoid(x):
    return jax.nn.sigmoid(x)

def _layernorm(x, axis=-1, eps=1e-05):
    m = jnp.mean(x, axis=axis, keepdims=True)
    v = jnp.var(x, axis=axis, keepdims=True)
    return (x - m) / jnp.sqrt(v + eps)

def _scatter_add(tgt, idx, src, axis=0):
    return tgt.at[idx].add(src)

def _segment_sum(src, seg, n):
    return jax.ops.segment_sum(src, seg, n)
kernel_name = 'mk_sandwich_d1_jaxref_r8_91a45b'

def setup_inputs(seed: int=0):
    np.random.seed(seed)
    _w = jnp.asarray

    def _L0_attn_setup():
        import jax, jax.numpy as jnp
        import numpy as np
        HIDDEN = 512
        NH = 32
        NKV = 8
        HD = 128
        GS = 128
        BASE = 10000.0
        B, S = (2, 256)

        def _dequant(codes, scales):
            w = codes.astype(jnp.float32) - 8.0
            return w * jnp.repeat(scales, GS, axis=0)

        def _rope(x):
            s, d = (x.shape[2], x.shape[3])
            pos = jnp.arange(s, dtype=jnp.float32)
            inv_freq = 1.0 / BASE ** (jnp.arange(0, d, 2, dtype=jnp.float32) / d)
            f = pos[:, None] * inv_freq[None, :]
            cos = jnp.cos(f)[None, None]
            sin = jnp.sin(f)[None, None]
            xe = x[..., ::2]
            xo = x[..., 1::2]
            re = xe * cos - xo * sin
            ro = xo * cos + xe * sin
            return jnp.stack([re, ro], axis=-1).reshape(x.shape)
        key = jax.random.key(seed)
        ks = jax.random.split(key, 9)

        def codes(k, i, o):
            return jax.random.randint(k, (i, o), 0, 16, dtype=jnp.int32)

        def scales(k, i, o):
            return jax.random.uniform(k, (i // GS, o), dtype=jnp.float32) * 0.02
        return {'hidden_states': jax.random.normal(ks[0], (B, S, HIDDEN), jnp.float32), 'q_codes': codes(ks[1], HIDDEN, NH * HD), 'q_scales': scales(ks[2], HIDDEN, NH * HD), 'k_codes': codes(ks[3], HIDDEN, NKV * HD), 'k_scales': scales(ks[4], HIDDEN, NKV * HD), 'v_codes': codes(ks[5], HIDDEN, NKV * HD), 'v_scales': scales(ks[6], HIDDEN, NKV * HD), 'o_codes': codes(ks[7], NH * HD, HIDDEN), 'o_scales': scales(ks[8], NH * HD, HIDDEN)}
    _L0_attn_in = _L0_attn_setup()

    def _L0_ffn_setup():
        import jax, jax.numpy as jnp
        import numpy as np
        D_MODEL = 512
        D_FF = 1376

        def _dequant_linear(x, w_int, scale):
            return jnp.einsum('bsd,fd->bsf', x, w_int.astype(x.dtype)) * scale
        key = jax.random.key(seed)
        ks = jax.random.split(key, 7)
        x = jax.random.normal(ks[0], (2, 256, D_MODEL), dtype=jnp.float32)
        gate_w = jax.random.randint(ks[1], (D_FF, D_MODEL), -127, 127, dtype=jnp.int32)
        up_w = jax.random.randint(ks[2], (D_FF, D_MODEL), -127, 127, dtype=jnp.int32)
        down_w = jax.random.randint(ks[3], (D_MODEL, D_FF), -127, 127, dtype=jnp.int32)
        gate_s = jax.random.uniform(ks[4], (D_FF,), dtype=jnp.float32) * 0.01 + 0.001
        up_s = jax.random.uniform(ks[5], (D_FF,), dtype=jnp.float32) * 0.01 + 0.001
        down_s = jax.random.uniform(ks[6], (D_MODEL,), dtype=jnp.float32) * 0.01 + 0.001
        return {'x': x, 'gate_w': gate_w, 'gate_s': gate_s, 'up_w': up_w, 'up_s': up_s, 'down_w': down_w, 'down_s': down_s}
    _L0_ffn_in = _L0_ffn_setup()
    _d = {'L0_attn_hidden_states': _L0_attn_in['hidden_states'], 'L0_attn_q_codes': _L0_attn_in['q_codes'], 'L0_attn_q_scales': _L0_attn_in['q_scales'], 'L0_attn_k_codes': _L0_attn_in['k_codes'], 'L0_attn_k_scales': _L0_attn_in['k_scales'], 'L0_attn_v_codes': _L0_attn_in['v_codes'], 'L0_attn_v_scales': _L0_attn_in['v_scales'], 'L0_attn_o_codes': _L0_attn_in['o_codes'], 'L0_attn_o_scales': _L0_attn_in['o_scales'], 'L0_ffn_gate_w': _L0_ffn_in['gate_w'], 'L0_ffn_gate_s': _L0_ffn_in['gate_s'], 'L0_ffn_up_w': _L0_ffn_in['up_w'], 'L0_ffn_up_s': _L0_ffn_in['up_s'], 'L0_ffn_down_w': _L0_ffn_in['down_w'], 'L0_ffn_down_s': _L0_ffn_in['down_s']}
    _x0 = _d['L0_attn_hidden_states']
    _d['L0_attn_hidden_states'] = jax.random.normal(jax.random.fold_in(jax.random.key(seed), 1), (4, 512, 512), dtype=_x0.dtype)
    del _x0
    return _d

def reference(L0_attn_hidden_states, L0_attn_q_codes, L0_attn_q_scales, L0_attn_k_codes, L0_attn_k_scales, L0_attn_v_codes, L0_attn_v_scales, L0_attn_o_codes, L0_attn_o_scales, L0_ffn_gate_w, L0_ffn_gate_s, L0_ffn_up_w, L0_ffn_up_s, L0_ffn_down_w, L0_ffn_down_s):

    def _L0_attn_ref(hidden_states, q_codes, q_scales, k_codes, k_scales, v_codes, v_scales, o_codes, o_scales):
        import jax, jax.numpy as jnp
        import numpy as np
        HIDDEN = 512
        NH = 32
        NKV = 8
        HD = 128
        GS = 128
        BASE = 10000.0
        B, S = (2, 256)

        def _dequant(codes, scales):
            w = codes.astype(jnp.float32) - 8.0
            return w * jnp.repeat(scales, GS, axis=0)

        def _rope(x):
            s, d = (x.shape[2], x.shape[3])
            pos = jnp.arange(s, dtype=jnp.float32)
            inv_freq = 1.0 / BASE ** (jnp.arange(0, d, 2, dtype=jnp.float32) / d)
            f = pos[:, None] * inv_freq[None, :]
            cos = jnp.cos(f)[None, None]
            sin = jnp.sin(f)[None, None]
            xe = x[..., ::2]
            xo = x[..., 1::2]
            re = xe * cos - xo * sin
            ro = xo * cos + xe * sin
            return jnp.stack([re, ro], axis=-1).reshape(x.shape)
        b, s, _ = hidden_states.shape
        q = hidden_states @ _dequant(q_codes, q_scales)
        k = hidden_states @ _dequant(k_codes, k_scales)
        v = hidden_states @ _dequant(v_codes, v_scales)
        q = q.reshape(b, s, NH, HD).transpose(0, 2, 1, 3)
        k = k.reshape(b, s, NKV, HD).transpose(0, 2, 1, 3)
        v = v.reshape(b, s, NKV, HD).transpose(0, 2, 1, 3)
        q = _rope(q)
        k = _rope(k)
        rf = NH // NKV
        k = jnp.repeat(k, rf, axis=1)
        v = jnp.repeat(v, rf, axis=1)
        scale = HD ** (-0.5)
        causal = jnp.tril(jnp.ones((s, s), dtype=bool))
        mask = jnp.where(causal, 0.0, -jnp.inf).astype(q.dtype)
        scores = jnp.einsum('bhqd,bhkd->bhqk', q, k) * scale + mask[None, None]
        attn = jax.nn.softmax(scores, axis=-1)
        out = jnp.einsum('bhqk,bhkd->bhqd', attn, v)
        out = out.transpose(0, 2, 1, 3).reshape(b, s, NH * HD)
        return out @ _dequant(o_codes, o_scales)

    def _L0_ffn_ref(x, gate_w, gate_s, up_w, up_s, down_w, down_s):
        import jax, jax.numpy as jnp
        import numpy as np
        D_MODEL = 512
        D_FF = 1376

        def _dequant_linear(x, w_int, scale):
            return jnp.einsum('bsd,fd->bsf', x, w_int.astype(x.dtype)) * scale
        gate = jax.nn.silu(_dequant_linear(x, gate_w, gate_s))
        up = _dequant_linear(x, up_w, up_s)
        h = gate * up
        return _dequant_linear(h, down_w, down_s)
    x = L0_attn_hidden_states
    x = x + _layernorm(_L0_attn_ref(_layernorm(x, axis=-1), L0_attn_q_codes, L0_attn_q_scales, L0_attn_k_codes, L0_attn_k_scales, L0_attn_v_codes, L0_attn_v_scales, L0_attn_o_codes, L0_attn_o_scales), axis=-1)
    x = x + _layernorm(_L0_ffn_ref(_layernorm(x, axis=-1), L0_ffn_gate_w, L0_ffn_gate_s, L0_ffn_up_w, L0_ffn_up_s, L0_ffn_down_w, L0_ffn_down_s), axis=-1)
    return x

_drawn_inputs = setup_inputs


def setup_inputs(seed=0):
    import zlib

    import numpy as np

    out = dict(_drawn_inputs(seed))
    spreads = {}
    factors = {}
    for name, (base, spread) in spreads.items():
        noise = np.random.default_rng([zlib.crc32(name.encode()), seed]).standard_normal(out[name].shape)
        drawn = base * np.exp(spread * noise) if base else spread * noise
        out[name] = jnp.asarray(drawn.astype(out[name].dtype))
    for name, factor in factors.items():
        out[name] = (out[name] * factor).astype(out[name].dtype)
    return out
```

```python
from contextlib import ExitStack

import concourse.bass as bass
from concourse import mybir

F32 = mybir.dt.float32
F16 = mybir.dt.float16
I32 = mybir.dt.int32
ALU = mybir.AluOpType
ACT = mybir.ActivationFunctionType
AX = mybir.AxisListType.X

P = 128
NB, S, D = 4, 512, 512
NH, NKV, HD = 32, 8, 128
GS = 128
HG = NH // NKV
KT = D // P
TT = S // P
NT = NB * TT
UNITS = NKV * NB
QW, KW = HG * HD, HD
GW = QW + 2 * KW
DFF = 1376
FT = -(-DFF // P)
FLAST = DFF - (FT - 1) * P
EPS = 1e-5

X_UP = 16.0
W_UP = 1024.0
P_UP = 4096.0
O_UP = 16.0
H_DOWN = 1.0 / 16.0
QK_UP = 16.0
SCORE_SCALE = float(HD) ** -0.5 / (QK_UP * QK_UP)
MASKED = 32768.0

GROUPS = ((3,), (2,), (1, 0))
NG = len(GROUPS)
ORDER = tuple(i for g in GROUPS for i in g)
S_AT = {3: (0, 0), 2: (1, 0), 1: (2, 0), 0: (2, 256)}
T_AT = {3: (0, 0), 2: (1, 0), 1: (0, 0), 0: (0, 256)}
P_AT = {3: 0, 2: 512, 1: 896, 0: 1152}
DONE = (1, 2, 4)
PW = 1280

FULL = ((("K", "O0"), ("O1",)), (("O2", "V"), ("Q0",)), (("O3",), ("Q1",)), (("Q2",), ("Q3",)))
FIRST = ((("K",), ()), (("V",), ("Q0",)), ((), ("Q1",)), (("Q2",), ("Q3",)))
LAST = ((("O0",), ("O1",)), (("O2",), ()), (("O3",), ()), ((), ()))
START = ("K", "V", "Q0", "Q1", "Q2", "Q3")


TOTAL_PIECES = 10 * (UNITS - 1) + 2 + 2 * TT


def listed(slots):
    return tuple(x for a, b in slots for x in a + b)


def act_takes(piece):
    return 0 if piece[0] == "O" else 1 if piece == "V" else 2


def pieces_before(U):
    if isinstance(U, int) and U <= 0:
        return 6 * (U + 1)
    return 10 * U + 2


def act_before(U):
    return 11 * U + 11


def rope_index(V, piece):
    return 5 * V + (0 if piece == "K" else 1 + int(piece[1]))


def after(eng, sem, value):
    if isinstance(value, int) and value <= 0:
        return
    eng.wait_ge(sem, value)


def layer(nc, x, q_codes, q_scales, k_codes, k_scales, v_codes, v_scales, o_codes, o_scales,
          gate_t, gate_s, up_t, up_s, down_t, down_s, cos_t, sin_t, ident_in, mask_in, out):
    ctx = ExitStack()
    with ctx:
        def sem(name):
            return ctx.enter_context(nc.semaphore(name))

        def psum(name, shape):
            return ctx.enter_context(nc.psum_tensor(name, shape, F32))

        def sb(name, shape, dt, where=ctx):
            return where.enter_context(nc.sbuf_tensor(name, shape, dt))

        ps_s = psum("ps_s", [P, 3, 512])
        ps_o = psum("ps_o", [P, 512])
        ps_t = psum("ps_t", [P, 2, 512])
        ps_p = psum("ps_p", [P, 2, 512])
        gu_bank = [ps_s[:, 0, :], ps_s[:, 1, :], ps_s[:, 2, :], ps_o[:, :]]

        y = sb("y", [P, NT, D], F32)
        x_hi = sb("x_hi", [P, KT, NB * S], F16)
        x_lo = sb("x_lo", [P, KT, NB * S], F16)
        ident = sb("ident", [P, P], F32)
        stats = sb("stats", [P, 2, 6], F32)
        mv = sb("mv", [P, TT, 2], F32)
        ve = sb("ve", [P, TT], F32)
        rstd = sb("rstd", [P, TT], F32)
        minus_half = sb("minus_half", [P, TT], F32)

        att = ctx.enter_context(ExitStack())
        w_hi = sb("w_hi", [P, 2 * KT, GW], F16, att)
        w_lo = sb("w_lo", [P, 2 * KT, GW], F16, att)
        wo_hi = sb("wo_hi", [P, 2 * HG, D], F16, att)
        wo_lo = sb("wo_lo", [P, 2 * HG, D], F16, att)
        w_code = sb("w_code", [P, 2, GW], I32, att)
        w_scale = sb("w_scale", [P, 2, GW], F32, att)
        o_code = sb("o_code", [P, 2, D], I32, att)
        o_scale = sb("o_scale", [P, 2, D], F32, att)
        w_val = sb("w_val", [P, GW], F32, att)
        o_val = sb("o_val", [P, D], F32, att)
        k_hi = sb("k_hi", [P, 2, S], F16, att)
        k_lo = sb("k_lo", [P, 2, S], F16, att)
        v_hi = sb("v_hi", [P, 2, S], F16, att)
        v_lo = sb("v_lo", [P, 2, S], F16, att)
        q_hi = sb("q_hi", [P, HG, S], F16, att)
        q_lo = sb("q_lo", [P, HG, S], F16, att)
        swap = sb("swap", [P, 2, S], F32, att)
        rot = sb("rot", [P, 2, S], F32, att)
        prob = sb("prob", [P, 2, PW], F32, att)
        pt_hi = sb("pt_hi", [P, TT, S], F16, att)
        pt_lo = sb("pt_lo", [P, TT, S], F16, att)
        ot_hi = sb("ot_hi", [P, 2, HG, S], F16, att)
        ot_lo = sb("ot_lo", [P, 2, HG, S], F16, att)
        cos = sb("cos", [P, S], F32, att)
        sin = sb("sin", [P, S], F32, att)
        mask_f = sb("mask_f", [P, P], F32, att)
        big_id = sb("big_id", [P, P], F16, att)
        mask = sb("mask", [P, P], F16, att)
        neg_max = sb("neg_max", [P, 2, TT], F32, att)
        exp_bias = sb("exp_bias", [P, 2, TT], F32, att)
        exp_sum = sb("exp_sum", [P, 2, TT], F32, att)
        inv_sum = sb("inv_sum", [P, 2, TT], F32, att)
        ln_x = y
        att.close()

        gate_w = sb("gate_w", [P, KT, DFF], F16)
        up_w = sb("up_w", [P, KT, DFF], F16)
        down_w = sb("down_w", [P, FT, D], F16)
        stage = sb("stage", [P, FT * D], I32)
        gate_i = stage[:, 0:KT * DFF].rearrange("p (k f) -> p k f", k=KT)
        down_i = stage[:, :].rearrange("p (k d) -> p k d", k=FT)
        up_i = sb("up_i", [P, KT, DFF], I32)
        gate_f = sb("gate_f", [P, FT], F32)
        up_f = sb("up_f", [P, FT], F32)
        down_f = sb("down_f", [P, D], F32)
        xres = sb("xres", [P, 2, D], F32)
        xn = sb("xn", [P, 2, D], F32)
        silu = sb("silu", [P, 2, S], F32)
        hid = sb("hid", [P, 2, S], F32)
        h_hi = sb("h_hi", [P, FT, S], F16)
        h_lo = sb("h_lo", [P, FT, S], F16)
        z = sb("z", [P, TT, D], F32)

        x_in = [sem(f"x_in{b}") for b in range(NB)]
        const_in = sem("const_in")
        table_in = sem("table_in")
        w_in = [sem("w_in0"), sem("w_in1")]
        o_in = [sem("o_in0"), sem("o_in1")]
        pool_passed = sem("pool_passed")
        sp_passed = sem("sp_passed")
        half_set = sem("half_set")
        y_zero = sem("y_zero")
        mask_set = sem("mask_set")
        ln_stat = sem("ln_stat")
        ln_ve = sem("ln_ve")
        ln_rstd = sem("ln_rstd")
        ln_done = sem("ln_done")
        xt_ps = sem("xt_ps")
        xt_hi = sem("xt_hi")
        xt_lo = sem("xt_lo")
        w_cent = sem("w_cent")
        w_prod = sem("w_prod")
        w_hid = sem("w_hid")
        w_lod = sem("w_lod")
        o_cent = sem("o_cent")
        o_prod = sem("o_prod")
        o_hid = sem("o_hid")
        o_lod = sem("o_lod")
        piece_ps = sem("piece_ps")
        piece_act = sem("piece_act")
        piece_dve = sem("piece_dve")
        sin_done = sem("sin_done")
        rot_sum = sem("rot_sum")
        rot_hi = sem("rot_hi")
        rot_lo = sem("rot_lo")
        s_ps = sem("s_ps")
        max_done = sem("max_done")
        bias_done = sem("bias_done")
        exp_done = sem("exp_done")
        inv_done = sem("inv_done")
        norm_done = sem("norm_done")
        t_ps = sem("t_ps")
        pt_hid = sem("pt_hid")
        pt_lod = sem("pt_lod")
        ot_ps = sem("ot_ps")
        ot_hid = sem("ot_hid")
        ot_lod = sem("ot_lod")
        gate_in = sem("gate_in")
        up_in = sem("up_in")
        down_in = sem("down_in")
        sc_in = sem("sc_in")
        gate_cv = sem("gate_cv")
        up_cv = sem("up_cv")
        down_cv = sem("down_cv")
        sc_cv = sem("sc_cv")
        res_in = [sem("res_in0"), sem("res_in1")]
        m_stat = sem("m_stat")
        m_ve = sem("m_ve")
        m_rstd = sem("m_rstd")
        m_step = sem("m_step")
        m_res = sem("m_res")
        m_xn = sem("m_xn")
        m_xt = sem("m_xt")
        m_xhi = sem("m_xhi")
        m_xlo = sem("m_xlo")
        g_ps = sem("g_ps")
        u_ps = sem("u_ps")
        silu_done = sem("silu_done")
        hid_done = sem("hid_done")
        h_hid = sem("h_hid")
        h_lod = sem("h_lod")
        d_ps = sem("d_ps")
        z_done = sem("z_done")
        out_rdy = sem("out_rdy")
        out_dma = sem("out_dma")

        block = ctx.enter_context(nc.Block())

        @block.sync
        def _(sp):
            sp.dma_start(ident[:, :], ident_in).then_inc(const_in, 16)
            for b in range(NB):
                sp.dma_start(y[:, b * TT:(b + 1) * TT, :],
                             x[b].rearrange("(t p) d -> p t d", p=P)).then_inc(x_in[b], 16)

            def load_w(n, buf):
                after(sp, w_prod, n - 1)
                sp.sem_inc(sp_passed)
                G, k = (n >> 2) & (NKV - 1), n & (KT - 1)
                for codes, scales, at, width in ((q_codes, q_scales, 0, QW), (k_codes, k_scales, QW, KW),
                                                 (v_codes, v_scales, QW + KW, KW)):
                    sp.dma_start(w_code[:, buf, at:at + width],
                                 codes[bass.ds(k * P, P), bass.ds(G * width, width)]).then_inc(w_in[buf], 16)
                    sp.dma_start(w_scale[:, buf, at:at + width],
                                 scales[bass.ds(k, 1), bass.ds(G * width, width)].to_broadcast([P, width])
                                 ).then_inc(w_in[buf], 16)

            def load_o(m, buf):
                after(sp, o_prod, m - 1)
                sp.sem_inc(sp_passed)
                H = m & (NH - 1)
                sp.dma_start(o_code[:, buf, :], o_codes[bass.ds(H * P, P), :]).then_inc(o_in[buf], 16)
                sp.dma_start(o_scale[:, buf, :],
                             o_scales[bass.ds(H, 1), :].to_broadcast([P, D])).then_inc(o_in[buf], 16)

            for n in range(2):
                load_w(n, n)
            for t, src in ((cos, cos_t), (sin, sin_t), (mask_f, mask_in)):
                sp.dma_start(t[:, :], src).then_inc(table_in, 16)
            for n in range(2, 6):
                load_w(n, n % 2)
            for m in range(4):
                load_o(m, m % 2)

            def unit(U, r):
                load_w(U + 6, r % 2)
                load_o(U + 4, r % 2)

            for r in range(2):
                unit(r, r)
            with sp.Fori(1, UNITS // 2 - 1) as p:
                for r in range(2):
                    unit(2 * p + r, r)

            sp.wait_ge(ot_lod, NH * NB)
            sp.wait_ge(piece_ps, TOTAL_PIECES)
            sp.wait_ge(piece_dve, TOTAL_PIECES)
            sp.dma_start(gate_i[:, :, :], gate_t.rearrange("(k p) f -> p k f", p=P)).then_inc(gate_in, 16)
            sp.dma_start(up_i[:, :, :], up_t.rearrange("(k p) f -> p k f", p=P)).then_inc(up_in, 16)
            full = (FT - 1) * P
            full = (FT - 1) * P
            with nc.allow_non_contiguous_dma(reason="one scale of a partition each, 1376 of them"):
                for t, src in ((gate_f, gate_s), (up_f, up_s)):
                    sp.dma_start(t[:, 0:FT - 1], src[0:full].rearrange("(k p) -> p k", p=P)).then_inc(sc_in, 16)
                    sp.dma_start(t[0:FLAST, FT - 1:FT], src[full:DFF].rearrange("(p a) -> p a", a=1)).then_inc(sc_in, 16)
            sp.dma_start(down_f[:, :], down_s.rearrange("(a d) -> a d", a=1).to_broadcast([P, D])).then_inc(sc_in, 16)

            def load_res(t):
                after(sp, m_res, t - 1)
                sp.dma_start(xres[:, t % 2, :], x[t // TT, (t % TT) * P:(t % TT + 1) * P, :]).then_inc(res_in[t % 2], 16)

            for t in range(2):
                load_res(t)
            sp.wait_ge(gate_cv, KT)
            sp.dma_start(down_i[:, 0:FT - 1, :],
                         down_t[0:full, :].rearrange("(k p) f -> p k f", p=P)).then_inc(down_in, 16)
            sp.dma_start(down_i[0:FLAST, FT - 1, :], down_t[full:DFF, :]).then_inc(down_in, 16)
            for t in range(2, TT):
                load_res(t)
            for c in range(NB):
                if c + 1 < NB:
                    for i in range(TT):
                        load_res((c + 1) * TT + i)
                for i in range(TT):
                    t = c * TT + i
                    sp.wait_ge(out_rdy, t + 1)
                    sp.dma_start(out[t // TT, (t % TT) * P:(t % TT + 1) * P, :], y[:, t, :]).then_inc(out_dma, 16)
            sp.wait_ge(out_dma, 16 * NT)

        @block.gpsimd
        def _(pool):
            pool.memset(minus_half[:, :], -0.5).then_inc(half_set, 1)
            pool.wait_ge(half_set, 1)

            def dequant_w(n, buf):
                pool.wait_ge(w_in[buf], 96 * ((n >> 1) + 1))
                after(pool, w_lod, n)
                pool.sem_inc(pool_passed)
                pool.tensor_scalar(w_val[:, :], w_code[:, buf, :], -8.0, W_UP, ALU.add, ALU.mult).then_inc(w_cent, 1)
                pool.wait_ge(w_cent, n + 1)
                pool.tensor_tensor(w_val[:, :], w_val[:, :], w_scale[:, buf, :], ALU.mult).then_inc(w_prod, 1)

            def dequant_o(m, buf):
                pool.wait_ge(o_in[buf], 32 * ((m >> 1) + 1))
                after(pool, o_lod, m)
                pool.sem_inc(pool_passed)
                pool.tensor_scalar(o_val[:, :], o_code[:, buf, :], -8.0, W_UP, ALU.add, ALU.mult).then_inc(o_cent, 1)
                pool.wait_ge(o_cent, m + 1)
                pool.tensor_tensor(o_val[:, :], o_val[:, :], o_scale[:, buf, :], ALU.mult).then_inc(o_prod, 1)

            def times_sin(V, vpar, piece, act_count):
                k = rope_index(V, piece)
                buf = rope_index(vpar, piece) % 2
                pool.wait_ge(piece_act, act_count)
                pool.tensor_tensor(swap[:, buf, :], swap[:, buf, :], sin[:, :], ALU.mult).then_inc(sin_done, 1)

            def normalise(n, hp):
                pool.wait_ge(inv_done, n + 1)
                pool.sem_inc(pool_passed)
                for i in ORDER:
                    a = P_AT[i]
                    t = prob[:, hp, a:a + (i + 1) * P]
                    pool.tensor_scalar(t, t, inv_sum[:, hp, i:i + 1], P_UP, ALU.mult, ALU.mult).then_inc(norm_done, 1)

            for b in range(NB):
                dequant_w(b, b % 2)
                pool.wait_ge(ln_ve, b + 1)
                pool.tensor_tensor(rstd[:, :], ve[:, :], minus_half[:, :], ALU.pow).then_inc(ln_rstd, 1)
            pool.wait_ge(table_in, 48)
            done = 0
            for piece in START:
                done += act_takes(piece)
                if piece != "V":
                    times_sin(0, 0, piece, done)
            dequant_w(4, 0)
            for b in range(NB):
                pool.wait_ge(xt_lo, NT)
                pool.wait_ge(xt_ps, NT)
                pool.memset(y[:, b * TT:(b + 1) * TT, :], 0.0).then_inc(y_zero, 1)
            for m in range(3):
                dequant_o(m, m % 2)
            normalise(0, 0)

            def unit(U, r, slots, last=False):
                done = act_before(U)
                for h in range(HG):
                    before, behind = slots[h]
                    first = True
                    for piece in before + behind:
                        done = done + act_takes(piece)
                        if piece[0] in "KQ":
                            times_sin(U + 1, (r + 1) % 2, piece, done)
                        if first and not (last and h == HG - 1):
                            normalise(U * HG + h + 1, (h + 1) % 2)
                            first = False
                    if first and not (last and h == HG - 1):
                        normalise(U * HG + h + 1, (h + 1) % 2)
                    if h == 1 and not last:
                        dequant_w(U + 5, (r + 1) % 2)
                    if h == 2 and not last:
                        dequant_o(U + 3, (r + 1) % 2)

            unit(0, 0, FIRST)
            unit(1, 1, FULL)
            with pool.Fori(1, UNITS // 2 - 1) as p:
                for r in range(2):
                    unit(2 * p + r, r, FULL)
            unit(UNITS - 2, 0, FULL)
            unit(UNITS - 1, 1, LAST, last=True)

            for k in range(KT):
                pool.wait_ge(up_in, 16)
                pool.tensor_copy(up_w[:, k, :], up_i[:, k, :]).then_inc(up_cv, 1)
            for norm in range(3 * NB):
                pool.wait_ge(m_ve, norm + 1)
                pool.tensor_tensor(rstd[:, :], ve[:, :], minus_half[:, :], ALU.pow).then_inc(m_rstd, 1)

        @block.scalar
        def _(act):
            act.wait_ge(table_in, 48)
            act.wait_ge(const_in, 16)
            act.activation(big_id[:, :], ident[:, :], ACT.Copy, scale=MASKED).then_inc(mask_set, 1)
            act.activation(mask[:, :], mask_f[:, :], ACT.Copy, scale=-MASKED).then_inc(mask_set, 1)

            def w_high(n):
                act.wait_ge(w_prod, n + 1)
                act.activation(w_hi[:, bass.ds(n & (2 * KT - 1), 1), :].rearrange("p a w -> p (a w)"),
                               w_val[:, :], ACT.Copy).then_inc(w_hid, 1)

            def o_high(m):
                act.wait_ge(o_prod, m + 1)
                act.activation(wo_hi[:, bass.ds(m & (2 * HG - 1), 1), :].rearrange("p a w -> p (a w)"),
                               o_val[:, :], ACT.Copy).then_inc(o_hid, 1)

            for t in range(NT):
                act.wait_ge(xt_ps, t + 1)
                act.activation(x_hi[:, :, t * P:(t + 1) * P], ps_t[:, t % 2, :].rearrange("p (k c) -> p k c", k=KT),
                               ACT.Copy, scale=X_UP).then_inc(xt_hi, 1)
                if t % 4 == 3:
                    w_high(t // 4)

            def rope_high(V, vpar, piece):
                k = rope_index(V, piece)
                buf = rope_index(vpar, piece) % 2
                if piece == "K":
                    dst = k_hi[:, vpar, :]
                    after(act, s_ps, (V - 1) * HG * NG)
                else:
                    h = int(piece[1])
                    dst = q_hi[:, h, :]
                    after(act, s_ps, ((V - 1) * HG + h + 1) * NG)
                act.wait_ge(rot_sum, k + 1)
                act.activation(dst, rot[:, buf, :], ACT.Copy).then_inc(rot_hi, 1)

            def piece_of(V, vpar, piece, bank, n, pending):
                if piece[0] in "KQ":
                    k = rope_index(V, piece)
                    buf = rope_index(vpar, piece) % 2
                    act.wait_ge(piece_ps, n + 1)
                    after(act, rot_sum, k - 1)
                    act.activation(swap[0:64, buf, :], ps_p[64:128, bank, :], ACT.Copy).then_inc(piece_act, 1)
                    act.activation(swap[64:128, buf, :], ps_p[0:64, bank, :], ACT.Copy).then_inc(piece_act, 1)
                elif piece == "V":
                    act.wait_ge(piece_ps, n + 1)
                    after(act, ot_ps, (V - 1) * HG)
                    act.activation(v_hi[:, vpar, :], ps_p[:, bank, :], ACT.Copy,
                                   scale=1.0 / (X_UP * W_UP)).then_inc(piece_act, 1)
                if pending:
                    rope_high(*pending)

            pending = None
            for j, piece in enumerate(START):
                piece_of(0, 0, piece, j % 2, j, pending)
                pending = (0, 0, piece) if piece[0] in "KQ" else None
            rope_high(*pending)
            w_high(4)

            def exps(n, hp):
                act.wait_ge(bias_done, n + 1)
                after(act, t_ps, (n - 1) * NG)
                for i in ORDER:
                    bank, col = S_AT[i]
                    w = (i + 1) * P
                    act.activation(prob[:, hp, P_AT[i]:P_AT[i] + w], ps_s[:, bank, col:col + w], ACT.Exp,
                                   bias=exp_bias[:, hp, i:i + 1], scale=SCORE_SCALE,
                                   accum_out=exp_sum[:, hp, i:i + 1]).then_inc(exp_done, 1)

            def pt_high(n, g):
                act.wait_ge(t_ps, n * NG + g + 1)
                after(act, ot_ps, n)
                for i in GROUPS[g]:
                    bank, col = T_AT[i]
                    act.activation(pt_hi[:, 0:i + 1, i * P:(i + 1) * P],
                                   ps_t[:, bank, col:col + (i + 1) * P].rearrange("p (j c) -> p j c", j=i + 1),
                                   ACT.Copy).then_inc(pt_hid, 1)

            def ot_high(n, r, h, before_u):
                act.wait_ge(ot_ps, n + 1)
                after(act, piece_ps, before_u)
                act.activation(ot_hi[:, r, h, :], ps_o[:, :], ACT.Copy, scale=O_UP / P_UP).then_inc(ot_hid, 1)

            exps(0, 0)
            for m in range(3):
                o_high(m)

            def unit(U, r, slots, pending, last=False):
                idx = 0
                for h in range(HG):
                    before, behind = slots[h]
                    n = U * HG + h
                    pt_high(n, 0)
                    pt_high(n, 1)
                    if not (last and h == HG - 1):
                        exps(n + 1, (h + 1) % 2)
                    for piece in before:
                        piece_of(U + 1, (r + 1) % 2, piece, idx % 2, pieces_before(U) + idx, pending)
                        pending = (U + 1, (r + 1) % 2, piece) if piece[0] in "KQ" else None
                        idx += 1
                    pt_high(n, 2)
                    for piece in behind:
                        piece_of(U + 1, (r + 1) % 2, piece, idx % 2, pieces_before(U) + idx, pending)
                        pending = (U + 1, (r + 1) % 2, piece) if piece[0] in "KQ" else None
                        idx += 1
                    ot_high(n, r, h, pieces_before(U) if not isinstance(U, int) or U >= 2 else 0)
                    if h == 2 and not last:
                        act.wait_ge(piece_ps, pieces_before(U))
                        w_high(U + 5)
                    if h == 3 and not last:
                        act.wait_ge(piece_ps, pieces_before(U))
                        o_high(U + 3)

            unit(0, 0, FIRST, None)
            unit(1, 1, FULL, (1, 1, "Q3"))
            with act.Fori(1, UNITS // 2 - 1) as p:
                for r in range(2):
                    unit(2 * p + r, r, FULL, (2 * p + r, r, "Q3"))
            unit(UNITS - 2, 0, FULL, (UNITS - 2, 0, "Q3"))
            unit(UNITS - 1, 1, LAST, (UNITS - 1, 1, "Q3"), last=True)

            act.wait_ge(sc_in, 80)
            act.mul(gate_f[:, 0:FT - 1], gate_f[:, 0:FT - 1], 1.0 / X_UP).then_inc(sc_cv, 1)
            act.mul(gate_f[0:FLAST, FT - 1:FT], gate_f[0:FLAST, FT - 1:FT], 1.0 / X_UP).then_inc(sc_cv, 1)
            act.mul(up_f[:, 0:FT - 1], up_f[:, 0:FT - 1], H_DOWN / X_UP).then_inc(sc_cv, 1)
            act.mul(up_f[0:FLAST, FT - 1:FT], up_f[0:FLAST, FT - 1:FT], H_DOWN / X_UP).then_inc(sc_cv, 1)
            act.mul(down_f[:, :], down_f[:, :], 1.0 / H_DOWN).then_inc(sc_cv, 1)
            for k in range(KT):
                act.wait_ge(gate_in, 16)
                act.activation(gate_w[:, k, :], gate_i[:, k, :], ACT.Copy).then_inc(gate_cv, 1)
            act.wait_ge(sc_cv, 5)

            def xt_high(c):
                for i in range(TT):
                    t = c * TT + i
                    act.wait_ge(m_xt, t + 1)
                    act.activation(x_hi[:, :, bass.ds(t * P, P)],
                                   ps_t[:, i % 2, :].rearrange("p (k c) -> p k c", k=KT),
                                   ACT.Copy, scale=X_UP).then_inc(m_xhi, 1)

            def hidden_high(c, f):
                j = c * FT + f
                rows = P if f < FT - 1 else FLAST
                act.wait_ge(hid_done, j + 1)
                after(act, d_ps, c * TT)
                act.activation(h_hi[0:rows, f, :], hid[0:rows, j % 2, :], ACT.Copy).then_inc(h_hid, 1)

            xt_high(0)
            for c in range(NB):
                for f in range(FT):
                    j = c * FT + f
                    rows = P if f < FT - 1 else FLAST
                    act.wait_ge(g_ps, j + 1)
                    after(act, hid_done, j - 1)
                    act.activation(silu[0:rows, j % 2, :], gu_bank[2 * (j % 2)][0:rows, :], ACT.Silu,
                                   scale=gate_f[0:rows, f:f + 1]).then_inc(silu_done, 1)
                    if f:
                        hidden_high(c, f - 1)
                hidden_high(c, FT - 1)
                if c + 1 < NB:
                    xt_high(c + 1)

        @block.tensor
        def _(pe):
            pe.wait_ge(const_in, 16)

            for t in range(NT):
                pe.wait_ge(ln_done, t + 1)
                after(pe, xt_lo, t - 1)
                after(pe, xt_hi, t - 1)
                for k in range(KT):
                    mm = pe.transpose(ps_t[:, t % 2, k * P:(k + 1) * P], ln_x[:, t, k * P:(k + 1) * P], ident[:, :])
                mm.then_inc(xt_ps, 1)

            def project(V, piece, bank):
                a = QW if piece == "K" else int(piece[1]) * HD
                w0 = ((V >> 2) & 1) * KT
                x0 = (V & (NB - 1)) * S
                for k in range(KT):
                    wh = w_hi[:, bass.ds(w0 + k, 1), a:a + HD].rearrange("p a w -> p (a w)")
                    wl = w_lo[:, bass.ds(w0 + k, 1), a:a + HD].rearrange("p a w -> p (a w)")
                    xh = x_hi[:, k, bass.ds(x0, S)]
                    xl = x_lo[:, k, bass.ds(x0, S)]
                    pe.matmul(ps_p[:, bank, :], wh, xh, start=(k == 0), stop=False)
                    pe.matmul(ps_p[:, bank, :], wh, xl, start=False, stop=False)
                    mm = pe.matmul(ps_p[:, bank, :], wl, xh, start=False, stop=(k == KT - 1))
                mm.then_inc(piece_ps, 1)

            def project_v(V, bank):
                w0 = ((V >> 2) & 1) * KT
                x0 = (V & (NB - 1)) * S
                a = QW + KW
                for i in range(TT):
                    o = ps_p[:, bank, i * HD:(i + 1) * HD]
                    for k in range(KT):
                        wh = w_hi[:, bass.ds(w0 + k, 1), a:a + HD].rearrange("p a w -> p (a w)")
                        wl = w_lo[:, bass.ds(w0 + k, 1), a:a + HD].rearrange("p a w -> p (a w)")
                        xh = x_hi[:, k, bass.ds(x0 + i * P, P)]
                        xl = x_lo[:, k, bass.ds(x0 + i * P, P)]
                        pe.matmul(o, xh, wh, start=(k == 0), stop=False)
                        pe.matmul(o, xh, wl, start=False, stop=False)
                        mm = pe.matmul(o, xl, wh, start=False, stop=(k == KT - 1))
                mm.then_inc(piece_ps, 1)

            def output(U, rprev, i, bank):
                w0 = ((U >> 2) & 1) * HG
                for h in range(HG):
                    wh = wo_hi[:, bass.ds(w0 + h, 1), :].rearrange("p a w -> p (a w)")
                    wl = wo_lo[:, bass.ds(w0 + h, 1), :].rearrange("p a w -> p (a w)")
                    oh = ot_hi[:, rprev, h, i * P:(i + 1) * P]
                    ol = ot_lo[:, rprev, h, i * P:(i + 1) * P]
                    pe.matmul(ps_p[:, bank, :], oh, wh, start=(h == 0), stop=False)
                    pe.matmul(ps_p[:, bank, :], oh, wl, start=False, stop=False)
                    mm = pe.matmul(ps_p[:, bank, :], ol, wh, start=False, stop=(h == HG - 1))
                mm.then_inc(piece_ps, 1)

            def scores(n, U, upar, h):
                pe.wait_ge(rot_hi, rope_index(U, f"Q{h}") + 1)
                pe.wait_ge(rot_lo, rope_index(U, f"Q{h}") + 1)
                after(pe, exp_done, n * TT)
                for group in GROUPS:
                    for i in group:
                        bank, col = S_AT[i]
                        w = (i + 1) * P
                        o = ps_s[:, bank, col:col + w]
                        qh, ql = q_hi[:, h, i * P:(i + 1) * P], q_lo[:, h, i * P:(i + 1) * P]
                        pe.matmul(o, qh, k_hi[:, upar, 0:w], start=True, stop=False)
                        pe.matmul(o, qh, k_lo[:, upar, 0:w], start=False, stop=False)
                        pe.matmul(o, ql, k_hi[:, upar, 0:w], start=False, stop=False)
                        mm = pe.matmul(ps_s[:, bank, col + i * P:col + w], big_id[:, :], mask[:, :],
                                       start=False, stop=True)
                    mm.then_inc(s_ps, 1)

            def transposes(n, hp, g):
                pe.wait_ge(norm_done, n * TT + DONE[g])
                free = n * TT + DONE[0] if g == 2 else n * TT
                after(pe, pt_hid, free)
                after(pe, pt_lod, free)
                for i in GROUPS[g]:
                    bank, col = T_AT[i]
                    for j in range(i + 1):
                        mm = pe.transpose(ps_t[:, bank, col + j * P:col + (j + 1) * P],
                                          prob[:, hp, P_AT[i] + j * P:P_AT[i] + (j + 1) * P], ident[:, :])
                mm.then_inc(t_ps, 1)

            def attend(n, U, upar, vcounts):
                pe.wait_ge(pt_hid, (n + 1) * TT)
                pe.wait_ge(pt_lod, (n + 1) * TT)
                pe.wait_ge(piece_act, vcounts[0])
                pe.wait_ge(piece_dve, vcounts[1])
                after(pe, ot_hid, n)
                after(pe, ot_lod, n)
                for j in range(TT):
                    o = ps_o[:, j * P:S]
                    vh, vl = v_hi[:, upar, j * HD:(j + 1) * HD], v_lo[:, upar, j * HD:(j + 1) * HD]
                    pe.matmul(o, vh, pt_hi[:, j, j * P:S], start=(j == 0), stop=False)
                    pe.matmul(o, vh, pt_lo[:, j, j * P:S], start=False, stop=False)
                    mm = pe.matmul(o, vl, pt_hi[:, j, j * P:S], start=False, stop=(j == TT - 1))
                mm.then_inc(ot_ps, 1)

            def do_piece(U, r, piece, idx, dve_free, act_free):
                after(pe, piece_dve, dve_free)
                after(pe, piece_act, act_free)
                if piece[0] == "O":
                    i = int(piece[1])
                    pe.wait_ge(ot_hid, U * HG)
                    pe.wait_ge(ot_lod, U * HG)
                    pe.wait_ge(o_hid, U + 3)
                    pe.wait_ge(o_lod, U + 3)
                    output(U - 1, (r + 1) % 2, i, idx % 2)
                else:
                    pe.wait_ge(w_hid, U + 5)
                    pe.wait_ge(w_lod, U + 5)
                    if piece == "V":
                        project_v(U + 1, idx % 2)
                    else:
                        project(U + 1, piece, idx % 2)

            pe.wait_ge(xt_hi, NT)
            pe.wait_ge(xt_lo, NT)
            for j, piece in enumerate(START):
                do_piece(-1, 1, piece, j, j - 1, sum(act_takes(q) for q in START[:max(0, j - 1)]))
            pe.wait_ge(mask_set, 2)
            scores(0, 0, 0, 0)

            def v_counts(U, slots):
                names = listed(slots)
                upto = names.index("V") + 1
                return (act_before(U - 1) + sum(map(act_takes, names[:upto])), pieces_before(U - 1) + upto)

            def unit(U, r, slots, prev_slots, last=False):
                names = listed(slots)
                vc = v_counts(U, prev_slots)
                idx = 0

                def run(pieces):
                    nonlocal idx
                    for piece in pieces:
                        act_free = act_before(U) - 2 if idx == 0 else \
                            act_before(U) + sum(map(act_takes, names[:max(0, idx - 1)]))
                        do_piece(U, r, piece, idx, pieces_before(U) + idx - 1, act_free)
                        idx += 1

                for h in range(HG):
                    n = U * HG + h
                    transposes(n, h % 2, 0)
                    transposes(n, h % 2, 1)
                    if h < HG - 1:
                        scores(n + 1, U, r, h + 1)
                    elif not last:
                        scores(n + 1, U + 1, (r + 1) % 2, 0)
                    run(slots[h][0])
                    transposes(n, h % 2, 2)
                    run(slots[h][1])
                    attend(n, U, r, vc)

            unit(0, 0, FIRST, ((START, ()),))
            unit(1, 1, FULL, FIRST)
            with pe.Fori(1, UNITS // 2 - 1) as p:
                for r in range(2):
                    unit(2 * p + r, r, FULL, FULL)
            unit(UNITS - 2, 0, FULL, FULL)
            unit(UNITS - 1, 1, LAST, FULL, last=True)

            base = pieces_before(UNITS - 1) + 4
            pe.wait_ge(ot_hid, UNITS * HG)
            pe.wait_ge(ot_lod, UNITS * HG)
            for i in range(TT):
                pe.wait_ge(piece_dve, base + i - 1)
                output(UNITS - 1, 1, i, i % 2)

            def xn_transposes(c):
                for i in range(TT):
                    t = c * TT + i
                    pe.wait_ge(m_xn, t + 1)
                    after(pe, m_xhi, t - 1)
                    after(pe, m_xlo, t - 1)
                    for k in range(KT):
                        mm = pe.transpose(ps_t[:, i % 2, k * P:(k + 1) * P], xn[:, i % 2, k * P:(k + 1) * P], ident[:, :])
                    mm.then_inc(m_xt, 1)

            xn_transposes(0)
            pe.wait_ge(gate_cv, KT)
            pe.wait_ge(up_cv, KT)
            for c in range(NB):
                pe.wait_ge(m_xhi, (c + 1) * TT)
                pe.wait_ge(m_xlo, (c + 1) * TT)
                for f in range(FT):
                    j = c * FT + f
                    rows = P if f < FT - 1 else FLAST
                    after(pe, silu_done, j - 1)
                    after(pe, hid_done, j - 1)
                    for w, bank, done in ((gate_w, 2 * (j % 2), g_ps), (up_w, 2 * (j % 2) + 1, u_ps)):
                        o = gu_bank[bank][0:rows, :]
                        for k in range(KT):
                            wk = w[:, k, f * P:f * P + rows]
                            pe.matmul(o, wk, x_hi[:, k, c * S:(c + 1) * S], start=(k == 0), stop=False)
                            mm = pe.matmul(o, wk, x_lo[:, k, c * S:(c + 1) * S], start=False, stop=(k == KT - 1))
                        mm.then_inc(done, 1)
                if c + 1 < NB:
                    xn_transposes(c + 1)
                pe.wait_ge(down_cv, 2)
                pe.wait_ge(h_hid, (c + 1) * FT)
                pe.wait_ge(h_lod, (c + 1) * FT)
                for i in range(TT):
                    t = c * TT + i
                    after(pe, z_done, t - 1)
                    if t < 2:
                        pe.wait_ge(piece_dve, base + TT)
                    for f in range(FT):
                        rows = P if f < FT - 1 else FLAST
                        w = down_w[0:rows, f, :]
                        pe.matmul(ps_p[:, t % 2, :], h_hi[0:rows, f, i * P:(i + 1) * P], w, start=(f == 0), stop=False)
                        mm = pe.matmul(ps_p[:, t % 2, :], h_lo[0:rows, f, i * P:(i + 1) * P], w,
                                       start=False, stop=(f == FT - 1))
                    mm.then_inc(d_ps, 1)

        @block.vector
        def _(dve):
            def stats_of(tile, i, done):
                dve.bn_stats(stats[:, i % 2, :], tile).then_inc(ln_stat, 1)
                dve.wait_ge(ln_stat, done + 1)
                dve.bn_aggr(mv[:, i, :], stats[:, i % 2, :]).then_inc(ln_stat, 1)

            def w_low(n):
                dve.wait_ge(w_hid, n + 1)
                at = bass.ds(n & (2 * KT - 1), 1)
                dve.tensor_tensor(w_lo[:, at, :].rearrange("p a w -> p (a w)"), w_val[:, :],
                                  w_hi[:, at, :].rearrange("p a w -> p (a w)"), ALU.subtract).then_inc(w_lod, 1)

            def o_low(m):
                dve.wait_ge(o_hid, m + 1)
                at = bass.ds(m & (2 * HG - 1), 1)
                dve.tensor_tensor(wo_lo[:, at, :].rearrange("p a w -> p (a w)"), o_val[:, :],
                                  wo_hi[:, at, :].rearrange("p a w -> p (a w)"), ALU.subtract).then_inc(o_lod, 1)

            for b in range(NB):
                dve.wait_ge(x_in[b], 16)
                for i in range(TT):
                    t = b * TT + i
                    stats_of(y[:, t, :], i, 2 * t)
                dve.wait_ge(ln_stat, 2 * TT * (b + 1))
                dve.tensor_scalar(ve[:, :], mv[:, :, 1], EPS, None, ALU.add).then_inc(ln_ve, 1)
                dve.wait_ge(ln_rstd, b + 1)
                for i in range(TT):
                    t = b * TT + i
                    dve.tensor_scalar(y[:, t, :], y[:, t, :], mv[:, i, 0:1], rstd[:, i:i + 1],
                                      ALU.subtract, ALU.mult).then_inc(ln_done, 1)
                for i in range(TT):
                    t = b * TT + i
                    dve.wait_ge(xt_hi, t + 1)
                    dve.scalar_tensor_tensor(x_lo[:, :, t * P:(t + 1) * P],
                                             ps_t[:, t % 2, :].rearrange("p (k c) -> p k c", k=KT), X_UP,
                                             x_hi[:, :, t * P:(t + 1) * P], ALU.mult, ALU.subtract).then_inc(xt_lo, 1)
                w_low(b)

            dve.wait_ge(table_in, 48)

            def rope_sum(V, vpar, piece, n):
                k, buf = rope_index(V, piece), rope_index(vpar, piece) % 2
                dve.wait_ge(sin_done, k + 1)
                dve.wait_ge(piece_dve, n + 1)
                dve.tensor_tensor(rot[:, buf, :], rot[:, buf, :], swap[:, buf, :], ALU.add).then_inc(rot_sum, 1)

            def rope_low(V, vpar, piece, n):
                k, buf = rope_index(V, piece), rope_index(vpar, piece) % 2
                hi, lo = (k_hi[:, vpar, :], k_lo[:, vpar, :]) if piece == "K" else \
                    (q_hi[:, int(piece[1]), :], q_lo[:, int(piece[1]), :])
                dve.wait_ge(rot_hi, k + 1)
                dve.tensor_tensor(lo, rot[:, buf, :], hi, ALU.subtract).then_inc(rot_lo, 1)

            def piece_of(V, vpar, piece, bank, n, done, pending):
                if pending:
                    rope_sum(*pending)
                dve.wait_ge(piece_ps, n + 1)
                if piece[0] in "KQ":
                    buf = rope_index(vpar, piece) % 2
                    after(dve, rot_lo, rope_index(V, piece) - 1)
                    dve.wait_ge(piece_act, done)
                    dve.tensor_tensor(rot[:, buf, :], ps_p[:, bank, :], cos[:, :], ALU.mult).then_inc(piece_dve, 1)
                elif piece == "V":
                    dve.wait_ge(piece_act, done)
                    dve.scalar_tensor_tensor(v_lo[:, vpar, :], ps_p[:, bank, :], 1.0 / (X_UP * W_UP),
                                             v_hi[:, vpar, :], ALU.mult, ALU.subtract).then_inc(piece_dve, 1)
                else:
                    add_output(V - 2, int(piece[1]), bank)
                if pending:
                    rope_low(*pending)

            def add_output(U, i, bank):
                t = bass.ds((U & (NB - 1)) * TT + i, 1)
                tile = y[:, t, :].rearrange("p a d -> p (a d)")
                dve.scalar_tensor_tensor(tile, ps_p[:, bank, :], 1.0 / (O_UP * W_UP), tile,
                                         ALU.mult, ALU.add).then_inc(piece_dve, 1)

            pending = None
            for j, piece in enumerate(START):
                piece_of(0, 0, piece, j % 2, j, sum(map(act_takes, START[:j + 1])), pending)
                pending = (0, 0, piece, j) if piece[0] in "KQ" else None
            rope_sum(*pending)
            rope_low(*pending)

            def maxima(n, hp):
                for g, group in enumerate(GROUPS):
                    dve.wait_ge(s_ps, n * NG + g + 1)
                    for i in group:
                        bank, col = S_AT[i]
                        dve.tensor_reduce(neg_max[:, hp, i:i + 1], ps_s[:, bank, col:col + (i + 1) * P], AX, ALU.max,
                                          negate=True).then_inc(max_done, 1)
                dve.wait_ge(max_done, (n + 1) * TT)
                after(dve, exp_done, (n - 1) * TT)
                dve.tensor_scalar(exp_bias[:, hp, :], neg_max[:, hp, :], SCORE_SCALE, None, ALU.mult).then_inc(bias_done, 1)

            def invert(n, hp):
                dve.wait_ge(exp_done, (n + 1) * TT)
                dve.reciprocal(inv_sum[:, hp, :], exp_sum[:, hp, :]).then_inc(inv_done, 1)

            def pt_low(n, g):
                dve.wait_ge(pt_hid, n * TT + DONE[g])
                for i in GROUPS[g]:
                    bank, col = T_AT[i]
                    dve.tensor_tensor(pt_lo[:, 0:i + 1, i * P:(i + 1) * P],
                                      ps_t[:, bank, col:col + (i + 1) * P].rearrange("p (j c) -> p j c", j=i + 1),
                                      pt_hi[:, 0:i + 1, i * P:(i + 1) * P], ALU.subtract).then_inc(pt_lod, 1)

            def ot_low(n, r, h):
                dve.wait_ge(ot_hid, n + 1)
                dve.scalar_tensor_tensor(ot_lo[:, r, h, :], ps_o[:, :], O_UP / P_UP, ot_hi[:, r, h, :],
                                         ALU.mult, ALU.subtract).then_inc(ot_lod, 1)

            w_low(4)
            maxima(0, 0)
            invert(0, 0)
            for m in range(3):
                o_low(m)
            dve.wait_ge(y_zero, NB)

            def unit(U, r, slots, pending, last=False):
                idx = 0
                names = listed(slots)
                vpar = (r + 1) % 2
                for h in range(HG):
                    before, behind = slots[h]
                    n = U * HG + h
                    more = not (last and h == HG - 1)
                    pt_low(n, 0)
                    pt_low(n, 1)
                    if more:
                        maxima(n + 1, (h + 1) % 2)
                    for j, piece in enumerate(before):
                        m = pieces_before(U) + idx
                        done = act_before(U) + sum(map(act_takes, names[:idx + 1]))
                        piece_of(U + 1, vpar, piece, idx % 2, m, done, pending)
                        pending = (U + 1, vpar, piece, m) if piece[0] in "KQ" else None
                        idx += 1
                        if j == 0 and more:
                            invert(n + 1, (h + 1) % 2)
                    if not before and more:
                        invert(n + 1, (h + 1) % 2)
                    pt_low(n, 2)
                    for piece in behind:
                        m = pieces_before(U) + idx
                        done = act_before(U) + sum(map(act_takes, names[:idx + 1]))
                        piece_of(U + 1, vpar, piece, idx % 2, m, done, pending)
                        pending = (U + 1, vpar, piece, m) if piece[0] in "KQ" else None
                        idx += 1
                    ot_low(n, r, h)
                    if h == 2 and not last:
                        w_low(U + 5)
                    if h == 3 and not last:
                        o_low(U + 3)

            unit(0, 0, FIRST, None)
            unit(1, 1, FULL, (1, 1, "Q3", pieces_before(1) - 1))
            with dve.Fori(1, UNITS // 2 - 1) as p:
                for r in range(2):
                    U = 2 * p + r
                    unit(U, r, FULL, (U, r, "Q3", pieces_before(U) - 1))
            unit(UNITS - 2, 0, FULL, (UNITS - 2, 0, "Q3", pieces_before(UNITS - 2) - 1))
            unit(UNITS - 1, 1, LAST, (UNITS - 1, 1, "Q3", pieces_before(UNITS - 1) - 1), last=True)
            base = pieces_before(UNITS - 1) + 4
            for i in range(TT):
                dve.wait_ge(piece_ps, base + i + 1)
                add_output(UNITS - 1, i, i % 2)

            step = [0]

            def link(ins):
                step[0] += 1
                ins.then_inc(m_step, 1)
                dve.wait_ge(m_step, step[0])

            norms = [0]

            def rstds(source):
                for i in range(TT):
                    link(dve.bn_stats(stats[:, i % 2, :], source(i)))
                    link(dve.bn_aggr(mv[:, i, :], stats[:, i % 2, :]))
                norms[0] += 1
                dve.tensor_scalar(ve[:, :], mv[:, :, 1], EPS, None, ALU.add).then_inc(m_ve, 1)
                dve.wait_ge(m_rstd, norms[0])

            def into_ffn(c):
                rstds(lambda i: y[:, c * TT + i, :])
                for i in range(TT):
                    t = c * TT + i
                    tile = y[:, t, :]
                    link(dve.tensor_scalar(tile, tile, mv[:, i, 0:1], rstd[:, i:i + 1], ALU.subtract, ALU.mult))
                    dve.wait_ge(res_in[t % 2], 16 * (t // 2 + 1))
                    dve.tensor_tensor(tile, tile, xres[:, t % 2, :], ALU.add).then_inc(m_res, 1)
                dve.wait_ge(m_res, (c + 1) * TT)
                rstds(lambda i: y[:, c * TT + i, :])
                for i in range(TT):
                    t = c * TT + i
                    after(dve, m_xt, t - 1)
                    dve.tensor_scalar(xn[:, i % 2, :], y[:, t, :], mv[:, i, 0:1], rstd[:, i:i + 1],
                                      ALU.subtract, ALU.mult).then_inc(m_xn, 1)
                    if i:
                        xn_low(t - 1)
                xn_low(c * TT + TT - 1)

            def xn_low(t):
                dve.wait_ge(m_xhi, t + 1)
                dve.scalar_tensor_tensor(x_lo[:, :, t * P:(t + 1) * P],
                                         ps_t[:, t % 2, :].rearrange("p (k c) -> p k c", k=KT), X_UP,
                                         x_hi[:, :, t * P:(t + 1) * P], ALU.mult, ALU.subtract).then_inc(m_xlo, 1)

            def hidden_low(c, f):
                j = c * FT + f
                rows = P if f < FT - 1 else FLAST
                dve.wait_ge(h_hid, j + 1)
                dve.tensor_tensor(h_lo[0:rows, f, :], hid[0:rows, j % 2, :], h_hi[0:rows, f, :],
                                  ALU.subtract).then_inc(h_lod, 1)

            into_ffn(0)
            dve.wait_ge(down_in, 32)
            dve.tensor_copy(down_w[:, 0:FT - 1, :], down_i[:, 0:FT - 1, :]).then_inc(down_cv, 1)
            dve.tensor_copy(down_w[0:FLAST, FT - 1, :], down_i[0:FLAST, FT - 1, :]).then_inc(down_cv, 1)
            dve.wait_ge(sc_cv, 5)
            for c in range(NB):
                for f in range(FT):
                    j = c * FT + f
                    rows = P if f < FT - 1 else FLAST
                    dve.wait_ge(silu_done, j + 1)
                    dve.wait_ge(u_ps, j + 1)
                    after(dve, h_lod, j - 1)
                    dve.scalar_tensor_tensor(hid[0:rows, j % 2, :], gu_bank[2 * (j % 2) + 1][0:rows, :],
                                             up_f[0:rows, f:f + 1], silu[0:rows, j % 2, :],
                                             ALU.mult, ALU.mult).then_inc(hid_done, 1)
                    if f:
                        hidden_low(c, f - 1)
                hidden_low(c, FT - 1)
                if c + 1 < NB:
                    into_ffn(c + 1)
                for i in range(TT):
                    t = c * TT + i
                    dve.wait_ge(d_ps, t + 1)
                    dve.tensor_tensor(z[:, i, :], ps_p[:, t % 2, :], down_f[:, :], ALU.mult).then_inc(z_done, 1)
                dve.wait_ge(z_done, (c + 1) * TT)
                rstds(lambda i: z[:, i, :])
                for i in range(TT):
                    t = c * TT + i
                    link(dve.tensor_scalar(z[:, i, :], z[:, i, :], mv[:, i, 0:1], rstd[:, i:i + 1], ALU.subtract, ALU.mult))
                    dve.tensor_tensor(y[:, t, :], y[:, t, :], z[:, i, :], ALU.add).then_inc(out_rdy, 1)


def rope_tables():
    import numpy as np
    f32 = np.float32
    inv = f32(1.0) / f32(10000.0) ** (np.arange(0, HD, 2, dtype=f32) / f32(HD))
    angle = np.arange(S, dtype=f32)[:, None] * inv[None, :]
    up = f32(QK_UP / (X_UP * W_UP))
    cos, sin = np.cos(angle).T * up, np.sin(angle).T * up
    return np.concatenate([cos, cos]).astype(f32), np.concatenate([-sin, sin]).astype(f32)


def halves(a):
    import numpy as np
    r, c = a.shape
    return np.ascontiguousarray(a.reshape(r, c // HD, HD // 2, 2).transpose(0, 1, 3, 2).reshape(r, c))


def kernel(**inputs):
    import numpy as np
    import concourse.bacc as bacc
    from concourse.bass_utils import run_bass_kernel_spmd

    given = {k.replace("L0_", "").replace("attn_", "").replace("ffn_", ""): np.asarray(v) for k, v in inputs.items()}
    cos, sin = rope_tables()
    arrays = {
        "x": given["hidden_states"],
        "q_codes": halves(given["q_codes"]), "q_scales": halves(given["q_scales"]),
        "k_codes": halves(given["k_codes"]), "k_scales": halves(given["k_scales"]),
        "v_codes": given["v_codes"], "v_scales": given["v_scales"],
        "o_codes": given["o_codes"], "o_scales": given["o_scales"],
        "gate_t": given["gate_w"].T, "gate_s": given["gate_s"],
        "up_t": given["up_w"].T, "up_s": given["up_s"],
        "down_t": given["down_w"].T, "down_s": given["down_s"],
        "cos_t": cos, "sin_t": sin,
        "ident_in": np.eye(P, dtype=np.float32), "mask_in": np.triu(np.ones((P, P), np.float32), 1),
    }
    arrays = {k: np.ascontiguousarray(v) for k, v in arrays.items()}
    nc = bacc.Bacc("TRN2", target_bir_lowering=False, num_devices=1)
    args = [nc.dram_tensor(k, v.shape, mybir.dt.from_np(v.dtype), kind="ExternalInput").ap() for k, v in arrays.items()]
    out = nc.dram_tensor("out", (NB, S, D), F32, kind="ExternalOutput").ap()
    layer(nc, *args, out)
    return run_bass_kernel_spmd(nc, [arrays], core_ids=[0]).results[0]["out"]
```

```python
from contextlib import ExitStack

import concourse.bass as bass
from concourse import mybir

F32 = mybir.dt.float32
F16 = mybir.dt.float16
I32 = mybir.dt.int32
ALU = mybir.AluOpType
ACT = mybir.ActivationFunctionType
AX = mybir.AxisListType.X

P = 128
NB, S, D = 4, 512, 512
NH, NKV, HD = 32, 8, 128
GS = 128
HG = NH // NKV
KT = D // P
TT = S // P
NT = NB * TT
UNITS = NKV * NB
QW, KW = HG * HD, HD
GW = QW + 2 * KW
DFF = 1376
FT = -(-DFF // P)
FLAST = DFF - (FT - 1) * P
EPS = 1e-5

X_UP = 16.0
W_UP = 1024.0
P_UP = 4096.0
O_UP = 16.0
H_DOWN = 1.0 / 16.0
QK_UP = 16.0
SCORE_SCALE = float(HD) ** -0.5 / (QK_UP * QK_UP)
MASKED = 32768.0

GROUPS = ((3,), (2,), (1, 0))
NG = len(GROUPS)
S_AT = {3: (0, 0), 2: (1, 0), 1: (2, 0), 0: (2, 256)}
T_AT = {3: (0, 0), 2: (1, 0), 1: (0, 0), 0: (0, 256)}
P_AT = {3: 0, 2: 512, 1: 896, 0: 1152}
PW = 1280
DONE = (1, 2, 4)

FULL = (("K",), ("V", "Q0"), ("Q1",), ("Q2", "Q3"))
LAST = (("Y0",), ("Y1",), ("Y2", "X0"), ("Y3", "X1"))
START = ("K", "V", "Q0", "Q1", "Q2", "Q3")


def sequence(slots):
    return tuple(x for pieces in slots for x in ("O0", "O1", "O2") + pieces + ("O3",))


def made(U, r, h, slots, back=0):
    if h < back:
        U, r, h, slots = U - 1, 1 - r, h + HG, FULL
    names, result = sequence(slots), []
    for piece in slots[h - back]:
        if piece[0] in "KVQ":
            at = names.index(piece)
            upto = [name for name in names[:at + 1] if name[0] in "KVQ"]
            result.append((U + 1, 1 - r, piece, at % 2, pieces_before(U) + len(upto),
                           act_before(U) + sum(map(act_takes, upto))))
    return result


def pieces_before(U):
    return len(START) * (U + 1)


def outs_before(U):
    return HG * KT * U - KT


def act_takes(piece):
    return 1 if piece == "V" else 2


def act_before(U):
    return sum(map(act_takes, START)) * (U + 1)


def rope_index(V, piece):
    return (HG + 1) * V + (0 if piece == "K" else 1 + int(piece[1]))


def after(eng, sem, value):
    if isinstance(value, int) and value <= 0:
        return
    eng.wait_ge(sem, value)


def flat(ap):
    return ap.rearrange("p a w -> p (a w)")


def layer(nc, x, w_codes, w_scales, o_codes, o_scales,
          gate_t, gate_s, up_t, up_s, down_t, down_s, cos_t, sin_t, ident_in, mask_in, out):
    ctx = ExitStack()
    with ctx:
        def sem(name):
            return ctx.enter_context(nc.semaphore(name))

        def psum(name, shape):
            return ctx.enter_context(nc.psum_tensor(name, shape, F32))

        def sb(name, shape, dt, where=ctx):
            return where.enter_context(nc.sbuf_tensor(name, shape, dt))

        ps_s = psum("ps_s", [P, 3, 512])
        ps_o = psum("ps_o", [P, 512])
        ps_t = psum("ps_t", [P, 2, 512])
        ps_p = psum("ps_p", [P, 2, 512])
        gu_bank = [ps_s[:, 0, :], ps_s[:, 1, :], ps_s[:, 2, :], ps_o[:, :]]

        row_bank = [ps_t[:, 0, :], ps_t[:, 1, :], ps_o[:, :]]
        y = sb("y", [P, NB, KT, S], F32)
        x_hi = sb("x_hi", [P, KT, NB * S], F16)
        x_lo = sb("x_lo", [P, KT, NB * S], F16)
        ffn_w = sb("ffn_w", [P, 2 * KT * DFF + FT * D], F16)
        gate_w = ffn_w[:, 0:KT * DFF].rearrange("p (k f) -> p k f", k=KT)
        up_w = ffn_w[:, KT * DFF:2 * KT * DFF].rearrange("p (k f) -> p k f", k=KT)
        down_w = ffn_w[:, 2 * KT * DFF:].rearrange("p (k d) -> p k d", k=FT)
        xs = ffn_w[:, 0:2 * NT * D].bitcast(F32).rearrange("p (t d) -> p t d", d=D)
        gate_f = sb("gate_f", [P, FT], F32)
        up_f = sb("up_f", [P, FT], F32)
        down_f = sb("down_f", [P, D], F32)
        ident = sb("ident", [P, P], F32)
        stats = sb("stats", [P, 4, 6], F32)
        mv = sb("mv", [P, 4, 2], F32)
        ve = sb("ve", [P, 4], F32)
        rstd = sb("rstd", [P, 4], F32)
        minus_half = sb("minus_half", [P, 4], F32)
        swap = sb("swap", [P, 2, S], F32)
        rot = sb("rot", [P, 2, S], F32)
        xres, xn = swap, rot

        att = ctx.enter_context(ExitStack())
        w_hi = sb("w_hi", [P, 2 * KT, GW], F16, att)
        w_lo = sb("w_lo", [P, 2 * KT, GW], F16, att)
        wo = sb("wo", [P, 2 * HG, D], F16, att)
        wo_scale = sb("wo_scale", [P, NH, KT], F32, att)
        w_code = sb("w_code", [P, 2, GW], I32, att)
        w_scale = sb("w_scale", [P, 2, GW], F32, att)
        o_code = sb("o_code", [P, 2, D], I32, att)
        w_val = sb("w_val", [P, GW], F32, att)
        k_hi = sb("k_hi", [P, 2, S], F16, att)
        k_lo = sb("k_lo", [P, 2, S], F16, att)
        v_hi = sb("v_hi", [P, 2, S], F16, att)
        v_lo = sb("v_lo", [P, 2, S], F16, att)
        q_hi = sb("q_hi", [P, HG, S], F16, att)
        q_lo = sb("q_lo", [P, HG, S], F16, att)
        prob = sb("prob", [P, 2, PW], F32, att)
        pt_hi = sb("pt_hi", [P, TT, S], F16, att)
        pt_lo = sb("pt_lo", [P, TT, S], F16, att)
        ot_hi = sb("ot_hi", [P, 2, S], F16, att)
        ot_lo = sb("ot_lo", [P, 2, S], F16, att)
        cos = sb("cos", [P, S], F32, att)
        sin = sb("sin", [P, S], F32, att)
        mask_f = sb("mask_f", [P, P], F32, att)
        big_id = sb("big_id", [P, P], F16, att)
        mask = sb("mask", [P, P], F16, att)
        neg_max = sb("neg_max", [P, 2, TT], F32, att)
        exp_bias = sb("exp_bias", [P, 2, TT], F32, att)
        exp_sum = sb("exp_sum", [P, 2, TT], F32, att)
        inv_sum = sb("inv_sum", [P, 2, TT], F32, att)
        att.close()

        silu = sb("silu", [P, 2, S], F32)
        hid = sb("hid", [P, 2, S], F32)
        h_hi = sb("h_hi", [P, FT, S], F16)
        h_lo = sb("h_lo", [P, FT, S], F16)
        z = sb("z", [P, TT, D], F32)

        x_in = [sem(f"x_in{b}") for b in range(NB)]
        x0_in = [sem(f"x0_in{i}") for i in range(TT)]
        const_in = sem("const_in")
        table_in = sem("table_in")
        w_in = [sem("w_in0"), sem("w_in1")]
        o_in = [sem("o_in0"), sem("o_in1")]
        ffn_in = sem("ffn_in")
        sc_in = sem("sc_in")
        res_in = [sem("res_in0"), sem("res_in1")]
        out_dma = [sem(f"out_dma{i}") for i in range(TT)]
        pool_passed = sem("pool_passed")
        sp_passed = sem("sp_passed")
        half_set = sem("half_set")
        y_zero = sem("y_zero")
        sc_cv = sem("sc_cv")
        mask_set = sem("mask_set")
        ln_stat = sem("ln_stat")
        ln_ve = sem("ln_ve")
        ln_rstd = sem("ln_rstd")
        ln_done = sem("ln_done")
        xt_ps = sem("xt_ps")
        xt_hi = sem("xt_hi")
        xt_lo = sem("xt_lo")
        w_cent = sem("w_cent")
        w_prod = sem("w_prod")
        w_hid = sem("w_hid")
        w_lod = sem("w_lod")
        o_cent = sem("o_cent")
        piece_ps = sem("piece_ps")
        piece_act = sem("piece_act")
        piece_dve = sem("piece_dve")
        sin_done = sem("sin_done")
        rot_sum = sem("rot_sum")
        rot_hi = sem("rot_hi")
        rot_lo = sem("rot_lo")
        s_ps = sem("s_ps")
        max_done = sem("max_done")
        bias_done = sem("bias_done")
        exp_done = sem("exp_done")
        inv_done = sem("inv_done")
        norm_done = sem("norm_done")
        t_ps = sem("t_ps")
        pt_hid = sem("pt_hid")
        pt_lod = sem("pt_lod")
        ot_ps = sem("ot_ps")
        ot_hid = sem("ot_hid")
        ot_lod = sem("ot_lod")
        o_ps = sem("o_ps")
        o_add = sem("o_add")
        y_ps = sem("y_ps")
        m_step = sem("m_step")
        m_ve = sem("m_ve")
        m_rstd = sem("m_rstd")
        y_read = sem("y_read")
        m_res = sem("m_res")
        m_xn = sem("m_xn")
        m_xt = sem("m_xt")
        m_xhi = sem("m_xhi")
        m_xlo = sem("m_xlo")
        g_ps = sem("g_ps")
        u_ps = sem("u_ps")
        silu_done = sem("silu_done")
        hid_done = sem("hid_done")
        h_hid = sem("h_hid")
        h_lod = sem("h_lod")
        d_ps = sem("d_ps")
        z_done = sem("z_done")
        out_rdy = sem("out_rdy")

        def rows_of(t):
            return y[:, t // TT, :, (t % TT) * P:(t % TT + 1) * P]

        def w_product(n):
            return prob[:, n % 2, 0:GW] if isinstance(n, int) and n < KT else w_val[:, :]

        block = ctx.enter_context(nc.Block())

        @block.sync
        def _(sp):
            def load_x(b):
                sp.dma_start(xs[:, b * TT:(b + 1) * TT, :],
                             x[b].rearrange("(t p) d -> p t d", p=P)).then_inc(x_in[b], 16)

            def load_w(n, buf):
                after(sp, w_prod, n - 1)
                sp.sem_inc(sp_passed)
                G, k = (n >> 2) & (NKV - 1), n & (KT - 1)
                sp.dma_start(w_code[:, buf, :],
                             w_codes[bass.ds(G, 1), bass.ds(k * P, P), :].rearrange("a p w -> p (a w)")
                             ).then_inc(w_in[buf], 16)
                sp.dma_start(w_scale[:, buf, :],
                             w_scales[bass.ds(G, 1), bass.ds(k, 1), :].rearrange("a k w -> (a k) w").to_broadcast([P, GW])
                             ).then_inc(w_in[buf], 16)

            def load_o(m, buf):
                after(sp, o_cent, m - 1)
                sp.sem_inc(sp_passed)
                H = m & (NH - 1)
                sp.dma_start(o_code[:, buf, :], o_codes[bass.ds(H * P, P), :]).then_inc(o_in[buf], 16)

            for i in range(TT):
                sp.dma_start(xs[:, i, :], x[0, i * P:(i + 1) * P, :]).then_inc(x0_in[i], 16)
            load_w(0, 0)
            sp.dma_start(ident[:, :], ident_in).then_inc(const_in, 16)
            load_w(1, 1)
            load_w(2, 0)
            load_w(3, 1)
            load_x(1)
            for t, src in ((cos, cos_t), (sin, sin_t), (mask_f, mask_in)):
                sp.dma_start(t[:, :], src).then_inc(table_in, 16)
            load_x(2)
            load_x(3)
            sp.dma_start(wo_scale[:, :, :], o_scales).then_inc(table_in, 16)
            for m in range(2):
                load_o(m, m)
            load_w(4, 0)
            load_w(5, 1)
            for m in range(2, 5):
                load_o(m, m % 2)
            for t, src in ((gate_f, gate_s), (up_f, up_s)):
                sp.dma_start(t[:, :], src).then_inc(sc_in, 16)
            sp.dma_start(down_f[:, :], down_s.rearrange("(a d) -> a d", a=1).to_broadcast([P, D])).then_inc(sc_in, 16)

            def unit(U, r):
                load_w(U + 6, r % 2)
                load_o(U + 5, (r + 1) % 2)

            with sp.Fori(0, UNITS // 2 - 1) as p:
                for r in range(2):
                    unit(2 * p + r, r)

            def load_res(t):
                after(sp, m_res, t - 1)
                sp.dma_start(xres[:, t % 2, :], x[t // TT, (t % TT) * P:(t % TT + 1) * P, :]).then_inc(res_in[t % 2], 16)

            sp.wait_ge(rot_sum, 5 * UNITS)
            for t in range(TT):
                load_res(t)
            for c in range(NB):
                if c + 1 < NB:
                    for i in range(TT):
                        load_res((c + 1) * TT + i)
                for i in range(TT):
                    t = c * TT + i
                    sp.wait_ge(out_rdy, t + 1)
                    sp.dma_start(out[t // TT, (t % TT) * P:(t % TT + 1) * P, :], z[:, i, :]).then_inc(out_dma[i], 16)
            for i in range(TT):
                sp.wait_ge(out_dma[i], 16 * NB)

        @block.gpsimd
        def _(pool):
            pool.memset(minus_half[:, :], -0.5).then_inc(half_set, 1)
            pool.wait_ge(half_set, 1)

            def rstd_batch(b):
                pool.wait_ge(ln_ve, b + 1)
                pool.tensor_tensor(rstd[:, :], ve[:, :], minus_half[:, :], ALU.pow).then_inc(ln_rstd, 1)

            def dequant_w(n, buf):
                pool.wait_ge(w_in[buf], 32 * ((n >> 1) + 1))
                after(pool, w_lod, n)
                pool.sem_inc(pool_passed)
                pool.tensor_scalar(w_val[:, :], w_code[:, buf, :], -8.0, 1.0, ALU.add, ALU.mult).then_inc(w_cent, 1)
                pool.wait_ge(w_cent, n - KT + 1)
                pool.tensor_tensor(w_val[:, :], w_val[:, :], w_scale[:, buf, :], ALU.mult).then_inc(w_prod, 1)

            def rotate(V, vpar, piece, acted, taken):
                buf = rope_index(vpar, piece) % 2
                pool.wait_ge(piece_act, acted)
                pool.tensor_tensor(swap[:, buf, :], swap[:, buf, :], sin[:, :], ALU.mult).then_inc(sin_done, 1)
                pool.wait_ge(piece_dve, taken)
                pool.wait_ge(sin_done, rope_index(V, piece) + 1)
                pool.tensor_tensor(rot[:, buf, :], rot[:, buf, :], swap[:, buf, :], ALU.add).then_inc(rot_sum, 1)

            def normalise(n, hp):
                pool.wait_ge(inv_done, n + 1)
                pool.sem_inc(pool_passed)
                for group in GROUPS:
                    for i in group:
                        a = P_AT[i]
                        t = prob[:, hp, a:a + (i + 1) * P]
                        pool.tensor_scalar(t, t, inv_sum[:, hp, i:i + 1], P_UP, ALU.mult, ALU.mult).then_inc(norm_done, 1)

            def start_piece(j):
                if START[j] != "V":
                    rotate(0, 0, START[j], sum(map(act_takes, START[:j + 1])), j + 1)

            for b in range(NB):
                pool.memset(y[:, b, :, :], 0.0).then_inc(y_zero, 1)
            rstd_batch(0)
            rstd_batch(1)
            pool.wait_ge(table_in, 64)
            start_piece(0)
            rstd_batch(2)
            start_piece(1)
            start_piece(2)
            start_piece(3)
            dequant_w(4, 0)
            rstd_batch(3)
            start_piece(4)
            normalise(0, 0)
            start_piece(5)

            def power(q):
                pool.wait_ge(m_ve, q + 1)
                pool.tensor_tensor(rstd[:, q % 4:q % 4 + 1], ve[:, q % 4:q % 4 + 1], minus_half[:, 0:1],
                                   ALU.pow).then_inc(m_rstd, 1)

            def unit(U, r, slots, last=False, first=False):
                for h in range(HG):
                    if not (first and h == 0):
                        for V, vpar, piece, bank, taken, acted in made(U, r, h, slots, 1):
                            if piece != "V":
                                rotate(V, vpar, piece, acted, taken)
                    if not (last and h == HG - 1):
                        normalise(U * HG + h + 1, (h + 1) % 2)
                    if last and h:
                        power(2 * h - 1)
                    if last:
                        power(2 * h)
                    if h == 1 and not last:
                        dequant_w(U + 5, (r + 1) % 2)

            unit(0, 0, FULL, first=True)
            unit(1, 1, FULL)
            pool.wait_ge(xt_lo, NT)
            pool.dma_start(gate_w[:, :, :], gate_t.rearrange("(k p) f -> p k f", p=P)).then_inc(ffn_in, 16)
            pool.dma_start(up_w[:, :, :], up_t.rearrange("(k p) f -> p k f", p=P)).then_inc(ffn_in, 16)
            full = (FT - 1) * P
            pool.dma_start(down_w[:, 0:FT - 1, :], down_t[0:full, :].rearrange("(k p) f -> p k f", p=P)).then_inc(ffn_in, 16)
            pool.dma_start(down_w[0:FLAST, FT - 1, :], down_t[full:DFF, :]).then_inc(ffn_in, 16)
            with pool.Fori(1, UNITS // 2 - 1) as p:
                for r in range(2):
                    unit(2 * p + r, r, FULL)
            unit(UNITS - 2, 0, FULL)
            unit(UNITS - 1, 1, LAST, last=True)
            for q in range(2 * TT - 1, 3 * NT):
                power(q)

        @block.scalar
        def _(act):
            def w_high(n):
                act.wait_ge(w_prod, n + 1)
                act.activation(flat(w_hi[:, bass.ds(n & (2 * KT - 1), 1), :]), w_product(n), ACT.Copy,
                               scale=W_UP).then_inc(w_hid, 1)

            def o_centre(m, buf):
                act.wait_ge(o_in[buf], 16 * ((m >> 1) + 1))
                act.activation(flat(wo[:, bass.ds(m & (2 * HG - 1), 1), :]), o_code[:, buf, :], ACT.Copy,
                               bias=-8.0).then_inc(o_cent, 1)

            def xt_high(b):
                for t in range(b * TT, (b + 1) * TT):
                    act.wait_ge(xt_ps, t + 1)
                    act.activation(x_hi[:, :, t * P:(t + 1) * P],
                                   row_bank[t % 3].rearrange("p (k c) -> p k c", k=KT),
                                   ACT.Copy, scale=X_UP).then_inc(xt_hi, 1)

            def rope_high(V, vpar, piece):
                buf = rope_index(vpar, piece) % 2
                if piece == "K":
                    dst = k_hi[:, vpar, :]
                    after(act, s_ps, (V - 1) * HG * NG)
                else:
                    dst = q_hi[:, int(piece[1]), :]
                    after(act, s_ps, ((V - 1) * HG + int(piece[1]) + 1) * NG)
                act.wait_ge(rot_sum, rope_index(V, piece) + 1)
                act.activation(dst, rot[:, buf, :], ACT.Copy).then_inc(rot_hi, 1)

            def take(V, vpar, piece, bank, n):
                act.wait_ge(piece_ps, n + 1)
                if piece == "V":
                    after(act, ot_ps, (V - 1) * HG)
                    act.activation(v_hi[:, vpar, :], ps_p[:, bank, :], ACT.Copy,
                                   scale=1.0 / (X_UP * W_UP)).then_inc(piece_act, 1)
                else:
                    buf = rope_index(vpar, piece) % 2
                    after(act, rot_sum, rope_index(V, piece) - 1)
                    act.activation(swap[0:64, buf, :], ps_p[64:128, bank, :], ACT.Copy).then_inc(piece_act, 1)
                    act.activation(swap[64:128, buf, :], ps_p[0:64, bank, :], ACT.Copy).then_inc(piece_act, 1)

            def start_piece(j):
                take(0, 0, START[j], j % 2, j)

            def start_rope(j):
                rope_high(0, 0, START[j])

            def exps(n, hp):
                act.wait_ge(bias_done, n + 1)
                after(act, t_ps, (n - 1) * NG)
                for group in GROUPS:
                    for i in group:
                        bank, col = S_AT[i]
                        w = (i + 1) * P
                        act.activation(prob[:, hp, P_AT[i]:P_AT[i] + w], ps_s[:, bank, col:col + w], ACT.Exp,
                                       bias=exp_bias[:, hp, i:i + 1], scale=SCORE_SCALE,
                                       accum_out=exp_sum[:, hp, i:i + 1]).then_inc(exp_done, 1)

            def pt_high(n, g):
                act.wait_ge(t_ps, n * NG + g + 1)
                after(act, ot_ps, n)
                for i in GROUPS[g]:
                    bank, col = T_AT[i]
                    act.activation(pt_hi[:, 0:i + 1, i * P:(i + 1) * P],
                                   ps_t[:, bank, col:col + (i + 1) * P].rearrange("p (j c) -> p j c", j=i + 1),
                                   ACT.Copy).then_inc(pt_hid, 1)

            def ot_high(n, hp):
                act.wait_ge(ot_ps, n + 1)
                after(act, o_ps, (n - 1) * KT)
                act.activation(ot_hi[:, hp, :], ps_o[:, :], ACT.Copy, scale=O_UP / P_UP).then_inc(ot_hid, 1)

            def rows_out(t, bank):
                act.wait_ge(y_ps, t + 1)
                act.activation(rows_of(t), bank.rearrange("p (k c) -> p k c", k=KT), ACT.Copy).then_inc(y_read, 1)

            def xn_high(t, bank):
                act.wait_ge(m_xt, t + 1)
                act.activation(x_hi[:, :, t * P:(t + 1) * P], bank.rearrange("p (k c) -> p k c", k=KT),
                               ACT.Copy, scale=X_UP).then_inc(m_xhi, 1)

            act.wait_ge(const_in, 16)
            act.activation(big_id[:, :], ident[:, :], ACT.Copy, scale=MASKED).then_inc(mask_set, 1)
            w_high(0)
            xt_high(0)
            for n in range(1, KT):
                w_high(n)
            start_piece(0)
            start_piece(1)
            xt_high(1)
            start_rope(0)
            start_piece(2)
            start_piece(3)
            xt_high(2)
            start_rope(2)
            act.wait_ge(table_in, 64)
            act.activation(mask[:, :], mask_f[:, :], ACT.Copy, scale=-MASKED).then_inc(mask_set, 1)
            act.mul(wo_scale[:, :, :], wo_scale[:, :, :], 1.0 / O_UP).then_inc(sc_cv, 1)
            start_piece(4)
            start_rope(3)
            for m in range(2):
                o_centre(m, m)
            w_high(4)
            xt_high(3)
            exps(0, 0)
            start_piece(5)
            start_rope(4)
            o_centre(2, 0)
            o_centre(3, 1)

            def ffn_scales():
                act.wait_ge(sc_in, 48)
                act.mul(gate_f[:, :], gate_f[:, :], 1.0 / X_UP).then_inc(sc_cv, 1)
                act.mul(up_f[:, :], up_f[:, :], H_DOWN / X_UP).then_inc(sc_cv, 1)
                act.mul(down_f[:, :], down_f[:, :], 1.0 / H_DOWN).then_inc(sc_cv, 1)

            def unit(U, r, slots, last=False, first=False):
                for h in range(HG):
                    n = U * HG + h
                    if h == 3 and not last:
                        after(act, o_ps, outs_before(U) + 4)
                        o_centre(U + 4, r % 2)
                    pt_high(n, 0)
                    if h == 2 and not last:
                        act.wait_ge(piece_ps, pieces_before(U))
                        w_high(U + 5)
                    pt_high(n, 1)
                    pt_high(n, 2)
                    if not (first and h == 0):
                        for V, vpar, piece, bank, taken, acted in made(U, r, h, slots, 1):
                            if piece != "V":
                                rope_high(V, vpar, piece)
                    else:
                        start_rope(5)
                    if not (last and h == HG - 1):
                        exps(n + 1, (h + 1) % 2)
                    for V, vpar, piece, bank, taken, acted in made(U, r, h, slots):
                        take(V, vpar, piece, bank, taken - 1)
                    for piece in slots[h]:
                        if piece[0] in "XY":
                            (xn_high if piece[0] == "X" else rows_out)(
                                int(piece[1]), ps_p[:, sequence(slots).index(piece) % 2, :])
                    ot_high(n, h % 2)

            unit(0, 0, FULL, first=True)
            unit(1, 1, FULL)
            with act.Fori(1, UNITS // 2 - 1) as p:
                for r in range(2):
                    unit(2 * p + r, r, FULL)
            ffn_scales()
            unit(UNITS - 2, 0, FULL)
            unit(UNITS - 1, 1, LAST, last=True)

            xn_high(TT - 2, ps_t[:, 0, :])
            xn_high(TT - 1, ps_t[:, 1, :])
            act.wait_ge(sc_cv, 4)

            def hidden_high(c, f):
                j = c * FT + f
                rows = P if f < FT - 1 else FLAST
                act.wait_ge(hid_done, j + 1)
                after(act, d_ps, c * TT)
                act.activation(h_hi[0:rows, f, :], hid[0:rows, j % 2, :], ACT.Copy).then_inc(h_hid, 1)

            for c in range(NB):
                for f in range(FT):
                    j = c * FT + f
                    rows = P if f < FT - 1 else FLAST
                    if c + 1 < NB and f in (0, 2, 4, 6):
                        rows_out((c + 1) * TT + f // 2, ps_t[:, 0, :])
                    if c + 1 < NB and f in (4, 6, 8, 10):
                        xn_high((c + 1) * TT + (f - 4) // 2, ps_t[:, 1, :])
                    act.wait_ge(g_ps, j + 1)
                    after(act, hid_done, j - 1)
                    act.activation(silu[0:rows, j % 2, :], gu_bank[2 * (j % 2)][0:rows, :], ACT.Silu,
                                   scale=gate_f[0:rows, f:f + 1]).then_inc(silu_done, 1)
                    if f:
                        hidden_high(c, f - 1)
                hidden_high(c, FT - 1)

        @block.tensor
        def _(pe):
            pe.wait_ge(const_in, 16)

            def xt(b):
                for t in range(b * TT, (b + 1) * TT):
                    pe.wait_ge(ln_done, t + 1)
                    after(pe, xt_lo, t - 2)
                    for k in range(KT):
                        mm = pe.transpose(row_bank[t % 3][:, k * P:(k + 1) * P], xs[:, t, k * P:(k + 1) * P], ident[:, :])
                    mm.then_inc(xt_ps, 1)

            def by_half(weights):
                return weights.rearrange("p (g k) w -> p g k w", g=2)

            def project(V, batch, piece, bank):
                a = QW if piece == "K" else int(piece[1]) * HD
                half = (V >> 2) & 1
                x0 = batch * S
                for k in range(KT):
                    if isinstance(V, int) and V == 0:
                        pe.wait_ge(w_lod, k + 1)
                    wh, wl = (flat(by_half(part)[:, bass.ds(half, 1), k, a:a + HD]) for part in (w_hi, w_lo))
                    xh, xl = x_hi[:, k, x0:x0 + S], x_lo[:, k, x0:x0 + S]
                    pe.matmul(ps_p[:, bank, :], wh, xh, start=(k == 0), stop=False)
                    pe.matmul(ps_p[:, bank, :], wh, xl, start=False, stop=False)
                    mm = pe.matmul(ps_p[:, bank, :], wl, xh, start=False, stop=(k == KT - 1))
                mm.then_inc(piece_ps, 1)

            def project_v(V, batch, bank):
                half = (V >> 2) & 1
                x0 = batch * S
                a = QW + KW
                for k in range(KT):
                    wh, wl = (flat(by_half(part)[:, bass.ds(half, 1), k, a:a + HD]) for part in (w_hi, w_lo))
                    for i in range(TT):
                        o = ps_p[:, bank, i * HD:(i + 1) * HD]
                        xh, xl = (part[:, k, x0 + i * P:x0 + (i + 1) * P] for part in (x_hi, x_lo))
                        pe.matmul(o, xh, wh, start=(k == 0 and i == 0), stop=False)
                        pe.matmul(o, xh, wl, start=False, stop=False)
                        mm = pe.matmul(o, xl, wh, start=False, stop=(k == KT - 1 and i == TT - 1))
                mm.then_inc(piece_ps, 1)

            def output(U, h, hp, nt, bank):
                w = flat(by_half(wo)[:, bass.ds((U >> 2) & 1, 1), h, nt * P:(nt + 1) * P])
                pe.matmul(ps_p[:, bank, :], w, ot_hi[:, hp, :], start=True, stop=False)
                pe.matmul(ps_p[:, bank, :], w, ot_lo[:, hp, :], start=False, stop=True).then_inc(o_ps, 1)

            def scores(n, U, upar, h, g):
                if g == 0:
                    pe.wait_ge(rot_lo, rope_index(U, f"Q{h}") + 1)
                    after(pe, exp_done, n * TT)
                for i in GROUPS[g]:
                    bank, col = S_AT[i]
                    w = (i + 1) * P
                    o = ps_s[:, bank, col:col + w]
                    qh, ql = q_hi[:, h, i * P:(i + 1) * P], q_lo[:, h, i * P:(i + 1) * P]
                    pe.matmul(o, qh, k_hi[:, upar, 0:w], start=True, stop=False)
                    pe.matmul(o, qh, k_lo[:, upar, 0:w], start=False, stop=False)
                    pe.matmul(o, ql, k_hi[:, upar, 0:w], start=False, stop=False)
                    mm = pe.matmul(ps_s[:, bank, col + i * P:col + w], big_id[:, :], mask[:, :],
                                   start=False, stop=True)
                mm.then_inc(s_ps, 1)

            def transposes(n, hp, g):
                pe.wait_ge(norm_done, n * TT + DONE[g])
                if g == 2:
                    pe.wait_ge(pt_lod, n * TT + DONE[0])
                for i in GROUPS[g]:
                    bank, col = T_AT[i]
                    for j in range(i + 1):
                        mm = pe.transpose(ps_t[:, bank, col + j * P:col + (j + 1) * P],
                                          prob[:, hp, P_AT[i] + j * P:P_AT[i] + (j + 1) * P], ident[:, :])
                mm.then_inc(t_ps, 1)

            def attend(n, U, upar, h):
                pe.wait_ge(pt_lod, (n + 1) * TT)
                if h == 0:
                    pe.wait_ge(piece_dve, pieces_before(U - 1) + 2)
                for j in range(TT):
                    o = ps_o[:, j * P:S]
                    vh, vl = v_hi[:, upar, j * HD:(j + 1) * HD], v_lo[:, upar, j * HD:(j + 1) * HD]
                    pe.matmul(o, vh, pt_hi[:, j, j * P:S], start=(j == 0), stop=False)
                    pe.matmul(o, vh, pt_lo[:, j, j * P:S], start=False, stop=False)
                    mm = pe.matmul(o, vl, pt_hi[:, j, j * P:S], start=False, stop=(j == TT - 1))
                mm.then_inc(ot_ps, 1)

            def turn_y(t, bank):
                for k in range(KT):
                    mm = pe.transpose(bank[:, k * P:(k + 1) * P],
                                      y[:, t // TT, k, (t % TT) * P:(t % TT + 1) * P], ident[:, :])
                mm.then_inc(y_ps, 1)

            def turn_xn(t, bank):
                pe.wait_ge(m_xn, t + 1)
                for k in range(KT):
                    mm = pe.transpose(bank[:, k * P:(k + 1) * P], xn[:, t % 2, k * P:(k + 1) * P], ident[:, :])
                mm.then_inc(m_xt, 1)

            def start_piece(j):
                after(pe, piece_dve, j - 1)
                if j == 0:
                    pe.wait_ge(xt_lo, TT)
                (project_v(0, 0, j % 2) if START[j] == "V" else project(0, 0, START[j], j % 2))

            xt(0)
            start_piece(0)
            start_piece(1)
            xt(1)
            start_piece(2)
            start_piece(3)
            xt(2)
            start_piece(4)
            pe.wait_ge(mask_set, 2)
            for g in range(NG):
                scores(0, 0, 0, 0, g)
            xt(3)
            start_piece(5)

            def unit(U, b, slots, last=False, first=False):
                r = b % 2
                names = sequence(slots)
                idx = 0

                def bank_free():
                    if first and idx < 5:
                        pe.wait_ge(piece_dve, len(START))
                        return
                    ahead = (sequence(FULL)[-2:] + names)[idx]
                    if idx < 2:
                        outs, pieces = outs_before(U), pieces_before(U)
                    else:
                        outs = outs_before(U) + sum(q[0] == "O" for q in names[:idx - 1])
                        pieces = pieces_before(U) + sum(q[0] in "KVQ" for q in names[:idx - 1])
                    if ahead[0] == "O":
                        after(pe, o_add, outs)
                    elif ahead[0] == "Y":
                        pe.wait_ge(y_read, int(ahead[1]) + 1)
                    elif ahead[0] == "X":
                        pe.wait_ge(m_xlo, int(ahead[1]) + 1)
                    else:
                        pe.wait_ge(piece_dve, pieces)

                def out_tile(n, h, nt):
                    nonlocal idx
                    if not (first and h == 0):
                        bank_free()
                        if nt == 0:
                            pe.wait_ge(ot_lod, n)
                        if h == 0:
                            output(U - 1, HG - 1, 1, nt, idx % 2)
                        else:
                            if b == 0 and h == 1 and nt == 0:
                                pe.wait_ge(o_cent, U + 4)
                            output(U, h - 1, (h - 1) % 2, nt, idx % 2)
                    idx += 1

                for h in range(HG):
                    n = U * HG + h
                    more = not (last and h == HG - 1)
                    nxt = (n + 1, U, r, h + 1) if h < HG - 1 else (n + 1, U + 1, (r + 1) % 2, 0)
                    if more:
                        scores(*nxt, 0)
                    if first and h == 0:
                        pe.wait_ge(xt_lo, NT)
                    transposes(n, h % 2, 0)
                    transposes(n, h % 2, 1)
                    if more:
                        scores(*nxt, 1)
                    out_tile(n, h, 0)
                    out_tile(n, h, 1)
                    if more:
                        scores(*nxt, 2)
                    transposes(n, h % 2, 2)
                    out_tile(n, h, 2)
                    for piece in slots[h]:
                        bank_free()
                        bank = ps_p[:, idx % 2, :]
                        if piece[0] == "Y":
                            turn_y(int(piece[1]), bank)
                        elif piece[0] == "X":
                            turn_xn(int(piece[1]), bank)
                        else:
                            if b == NB - 1 and piece == START[0]:
                                pe.wait_ge(w_lod, U + 5)
                            if piece == "V":
                                project_v(U + 1, (b + 1) % NB, idx % 2)
                            else:
                                project(U + 1, (b + 1) % NB, piece, idx % 2)
                        idx += 1
                    out_tile(n, h, 3)
                    attend(n, U, r, h)

            unit(0, 0, FULL, first=True)
            unit(1, 1, FULL)
            with pe.Fori(0, UNITS // NB - 1) as p:
                for i in range(NB):
                    unit(NB * p + 2 + i, (2 + i) % NB, FULL)
            unit(UNITS - 2, NB - 2, FULL)
            unit(UNITS - 1, NB - 1, LAST, last=True)

            outs = outs_before(UNITS) + KT

            def last_output(nt):
                if nt == 0:
                    pe.wait_ge(ot_lod, UNITS * HG)
                    pe.wait_ge(m_xlo, 2)
                pe.wait_ge(o_add, outs - 4 + max(0, nt - 1))
                output(UNITS - 1, HG - 1, 1, nt, nt % 2)

            turn_xn(TT - 2, ps_t[:, 0, :])
            last_output(0)
            last_output(1)
            turn_xn(TT - 1, ps_t[:, 1, :])
            last_output(2)
            last_output(3)
            pe.wait_ge(ffn_in, 64)
            for c in range(NB):
                for f in range(FT):
                    j = c * FT + f
                    rows = P if f < FT - 1 else FLAST
                    if f == 0:
                        pe.wait_ge(m_xlo, (c + 1) * TT)
                    if c + 1 < NB and f in (0, 2, 4, 6):
                        t = (c + 1) * TT + f // 2
                        pe.wait_ge(y_read, t)
                        if t == (NB - 1) * TT:
                            pe.wait_ge(o_add, outs)
                        turn_y(t, ps_t[:, 0, :])
                    if c + 1 < NB and f in (4, 6, 8, 10):
                        t = (c + 1) * TT + (f - 4) // 2
                        pe.wait_ge(m_xlo, t)
                        turn_xn(t, ps_t[:, 1, :])
                    after(pe, silu_done, j - 1)
                    after(pe, hid_done, j - 1)
                    for w, bank, done in ((gate_w, 2 * (j % 2), g_ps), (up_w, 2 * (j % 2) + 1, u_ps)):
                        o = gu_bank[bank][0:rows, :]
                        for k in range(KT):
                            wk = w[:, k, f * P:f * P + rows]
                            pe.matmul(o, wk, x_hi[:, k, c * S:(c + 1) * S], start=(k == 0), stop=False)
                            mm = pe.matmul(o, wk, x_lo[:, k, c * S:(c + 1) * S], start=False, stop=(k == KT - 1))
                        mm.then_inc(done, 1)
                for i in range(TT):
                    t = c * TT + i
                    after(pe, z_done, t - 1)
                    if t < 2:
                        pe.wait_ge(o_add, outs)
                    for f in range(FT):
                        rows = P if f < FT - 1 else FLAST
                        w = down_w[0:rows, f, :]
                        if i == 0:
                            pe.wait_ge(h_lod, c * FT + f + 1)
                        pe.matmul(ps_p[:, t % 2, :], h_hi[0:rows, f, i * P:(i + 1) * P], w, start=(f == 0), stop=False)
                        mm = pe.matmul(ps_p[:, t % 2, :], h_lo[0:rows, f, i * P:(i + 1) * P], w,
                                       start=False, stop=(f == FT - 1))
                    mm.then_inc(d_ps, 1)

        @block.vector
        def _(dve):
            def w_low(n):
                dve.wait_ge(w_hid, n + 1)
                at = bass.ds(n & (2 * KT - 1), 1)
                dve.scalar_tensor_tensor(flat(w_lo[:, at, :]), w_product(n), W_UP, flat(w_hi[:, at, :]),
                                         ALU.mult, ALU.subtract).then_inc(w_lod, 1)

            def dequant(n):
                dve.wait_ge(w_in[n % 2], 32 * (n // 2 + 1))
                after(dve, w_lod, n - 1)
                dve.scalar_tensor_tensor(w_product(n), w_code[:, n % 2, :], -8.0, w_scale[:, n % 2, :],
                                         ALU.add, ALU.mult).then_inc(w_prod, 1)

            def norm_stats(b):
                for i in range(TT):
                    dve.wait_ge(x_in[b], 16) if b else dve.wait_ge(x0_in[i], 16)
                    dve.bn_stats(stats[:, i, :], xs[:, b * TT + i, :]).then_inc(ln_stat, 1)
                for i in range(TT):
                    dve.wait_ge(ln_stat, 2 * TT * b + TT)
                    dve.bn_aggr(mv[:, i, :], stats[:, i, :]).then_inc(ln_stat, 1)
                dve.wait_ge(ln_stat, 2 * TT * (b + 1))
                dve.tensor_scalar(ve[:, :], mv[:, :, 1], EPS, None, ALU.add).then_inc(ln_ve, 1)

            def norm_rows(b):
                dve.wait_ge(ln_rstd, b + 1)
                for i in range(TT):
                    t = b * TT + i
                    dve.tensor_scalar(xs[:, t, :], xs[:, t, :], mv[:, i, 0:1], rstd[:, i:i + 1],
                                      ALU.subtract, ALU.mult).then_inc(ln_done, 1)

            def xt_low(b):
                for t in range(b * TT, (b + 1) * TT):
                    dve.wait_ge(xt_hi, t + 1)
                    dve.scalar_tensor_tensor(x_lo[:, :, t * P:(t + 1) * P],
                                             row_bank[t % 3].rearrange("p (k c) -> p k c", k=KT), X_UP,
                                             x_hi[:, :, t * P:(t + 1) * P], ALU.mult, ALU.subtract).then_inc(xt_lo, 1)

            def take(V, vpar, piece, bank, acted):
                dve.wait_ge(piece_act, acted)
                if piece == "V":
                    dve.scalar_tensor_tensor(v_lo[:, vpar, :], ps_p[:, bank, :], 1.0 / (X_UP * W_UP),
                                             v_hi[:, vpar, :], ALU.mult, ALU.subtract).then_inc(piece_dve, 1)
                else:
                    buf = rope_index(vpar, piece) % 2
                    after(dve, rot_lo, rope_index(V, piece) - 1)
                    dve.tensor_tensor(rot[:, buf, :], ps_p[:, bank, :], cos[:, :], ALU.mult).then_inc(piece_dve, 1)

            def rope_low(V, vpar, piece):
                buf = rope_index(vpar, piece) % 2
                hi, lo = (k_hi[:, vpar, :], k_lo[:, vpar, :]) if piece == "K" else \
                    (q_hi[:, int(piece[1]), :], q_lo[:, int(piece[1]), :])
                dve.wait_ge(rot_hi, rope_index(V, piece) + 1)
                dve.tensor_tensor(lo, rot[:, buf, :], hi, ALU.subtract).then_inc(rot_lo, 1)

            def start_piece(j):
                if j == 0:
                    dve.wait_ge(table_in, 64)
                take(0, 0, START[j], j % 2, sum(map(act_takes, START[:j + 1])))

            def start_rope(j):
                rope_low(0, 0, START[j])

            def add_output(U, b, h, nt, bank, n):
                dve.wait_ge(o_ps, n + 1)
                tile = y[:, b, nt, :]
                scale = wo_scale[:, bass.ds(((U >> 2) & (NKV - 1)) * HG + h, 1), nt]
                dve.scalar_tensor_tensor(tile, ps_p[:, bank, :], scale, tile, ALU.mult, ALU.add).then_inc(o_add, 1)

            def maxima(n, hp, g):
                dve.wait_ge(s_ps, n * NG + g + 1)
                for i in GROUPS[g]:
                    bank, col = S_AT[i]
                    dve.tensor_reduce(neg_max[:, hp, i:i + 1], ps_s[:, bank, col:col + (i + 1) * P], AX, ALU.max,
                                      negate=True).then_inc(max_done, 1)

            def bias(n, hp):
                dve.wait_ge(max_done, (n + 1) * TT)
                after(dve, exp_done, (n - 1) * TT)
                dve.tensor_scalar(exp_bias[:, hp, :], neg_max[:, hp, :], SCORE_SCALE, None, ALU.mult).then_inc(bias_done, 1)

            def invert(n, hp):
                dve.wait_ge(exp_done, (n + 1) * TT)
                dve.reciprocal(inv_sum[:, hp, :], exp_sum[:, hp, :]).then_inc(inv_done, 1)

            def pt_low(n, g):
                dve.wait_ge(pt_hid, n * TT + DONE[g])
                for i in GROUPS[g]:
                    bank, col = T_AT[i]
                    dve.tensor_tensor(pt_lo[:, 0:i + 1, i * P:(i + 1) * P],
                                      ps_t[:, bank, col:col + (i + 1) * P].rearrange("p (j c) -> p j c", j=i + 1),
                                      pt_hi[:, 0:i + 1, i * P:(i + 1) * P], ALU.subtract).then_inc(pt_lod, 1)

            def ot_low(n, hp):
                dve.wait_ge(ot_hid, n + 1)
                dve.scalar_tensor_tensor(ot_lo[:, hp, :], ps_o[:, :], O_UP / P_UP, ot_hi[:, hp, :],
                                         ALU.mult, ALU.subtract).then_inc(ot_lod, 1)

            norm_stats(0)
            dequant(0)
            norm_rows(0)
            dequant(1)
            w_low(0)
            xt_low(0)
            dequant(2)
            w_low(1)
            dequant(3)
            w_low(2)
            w_low(3)
            norm_stats(1)
            norm_rows(1)
            start_piece(0)
            start_piece(1)
            xt_low(1)
            start_rope(0)
            norm_stats(2)
            start_piece(2)
            norm_rows(2)
            start_piece(3)
            xt_low(2)
            start_rope(2)
            norm_stats(3)
            start_piece(4)
            norm_rows(3)
            start_rope(3)
            for g in range(NG):
                maxima(0, 0, g)
            bias(0, 0)
            w_low(4)
            xt_low(3)
            invert(0, 0)
            start_piece(5)
            start_rope(4)
            dve.wait_ge(y_zero, NB)
            dve.wait_ge(sc_cv, 1)

            step, asked = [0], [0]

            def link(ins):
                step[0] += 1
                ins.then_inc(m_step, 1)
                dve.wait_ge(m_step, step[0])

            def statistics(source):
                q = asked[0] % 4
                asked[0] += 1
                link(dve.bn_stats(stats[:, q, :], source))
                link(dve.bn_aggr(mv[:, q, :], stats[:, q, :]))
                dve.tensor_scalar(ve[:, q:q + 1], mv[:, q, 1:2], EPS, None, ALU.add).then_inc(m_ve, 1)

            def newest():
                dve.wait_ge(m_rstd, asked[0])
                return (asked[0] - 1) % 4

            def rows_first(t):
                dve.wait_ge(y_read, t + 1)
                statistics(rows_of(t))

            def rows_add(t):
                q = newest()
                link(dve.tensor_scalar(rows_of(t), rows_of(t), mv[:, q, 0:1], rstd[:, q:q + 1],
                                       ALU.subtract, ALU.mult))
                dve.wait_ge(res_in[t % 2], 16 * (t // 2 + 1))
                dve.tensor_tensor(rows_of(t), rows_of(t), xres[:, t % 2, :].rearrange("p (k c) -> p k c", k=KT),
                                  ALU.add).then_inc(m_res, 1)
                dve.wait_ge(m_res, t + 1)
                statistics(rows_of(t))

            def to_xn(t):
                q = newest()
                after(dve, m_xt, t - 1)
                dve.tensor_scalar(xn[:, t % 2, :].rearrange("p (k c) -> p k c", k=KT), rows_of(t), mv[:, q, 0:1],
                                  rstd[:, q:q + 1], ALU.subtract, ALU.mult).then_inc(m_xn, 1)

            def xn_low(t, bank):
                dve.wait_ge(m_xhi, t + 1)
                dve.scalar_tensor_tensor(x_lo[:, :, t * P:(t + 1) * P], bank.rearrange("p (k c) -> p k c", k=KT), X_UP,
                                         x_hi[:, :, t * P:(t + 1) * P], ALU.mult, ALU.subtract).then_inc(m_xlo, 1)

            def add_last(nt):
                add_output(UNITS - 1, NB - 1, HG - 1, nt, nt % 2, outs_before(UNITS) + nt)

            def unit(U, b, slots, last=False, first=False):
                r = b % 2
                names = sequence(slots)

                def out_tile(h, nt):
                    at = [i for i, name in enumerate(names) if name == f"O{nt}"][h]
                    before = outs_before(U) + h * KT + nt
                    if h:
                        add_output(U, b, h - 1, nt, at % 2, before)
                    elif not first:
                        add_output(U - 1, (b - 1) % NB, HG - 1, nt, at % 2, before)

                for h in range(HG):
                    n = U * HG + h
                    hp = (h + 1) % 2
                    more = not (last and h == HG - 1)
                    taken_now = made(U, r, h, slots)
                    early = taken_now[:-1] if len(slots[h]) == 2 and not last else []
                    if more:
                        maxima(n + 1, hp, 0)
                    pt_low(n, 0)
                    out_tile(h, 0)
                    out_tile(h, 1)
                    if more:
                        maxima(n + 1, hp, 1)
                        maxima(n + 1, hp, 2)
                        bias(n + 1, hp)
                    out_tile(h, 2)
                    pt_low(n, 1)
                    pt_low(n, 2)
                    if not (first and h == 0):
                        for V, vpar, piece, bank, taken, acted in made(U, r, h, slots, 1):
                            if piece != "V":
                                rope_low(V, vpar, piece)
                    else:
                        start_rope(5)
                    if more:
                        invert(n + 1, hp)
                    if last and h:
                        rows_add(h - 1)
                    if h == 3 and not last:
                        w_low(U + 5)
                    for V, vpar, piece, bank, taken, acted in early:
                        take(V, vpar, piece, bank, acted)
                    for piece in slots[h]:
                        if piece[0] == "X":
                            xn_low(int(piece[1]), ps_p[:, names.index(piece) % 2, :])
                    out_tile(h, 3)
                    for V, vpar, piece, bank, taken, acted in taken_now[len(early):]:
                        take(V, vpar, piece, bank, acted)
                    if last and h:
                        to_xn(h - 1)
                    if last and h == HG - 1:
                        ot_low(n, h % 2)
                        rows_first(h)
                        add_last(0)
                        rows_add(h)
                        add_last(1)
                        to_xn(h)
                    else:
                        if last:
                            rows_first(h)
                        ot_low(n, h % 2)

            unit(0, 0, FULL, first=True)
            unit(1, 1, FULL)
            with dve.Fori(0, UNITS // NB - 1) as p:
                for i in range(NB):
                    unit(NB * p + 2 + i, (2 + i) % NB, FULL)
            unit(UNITS - 2, NB - 2, FULL)
            unit(UNITS - 1, NB - 1, LAST, last=True)
            def hidden_low(c, f):
                j = c * FT + f
                rows = P if f < FT - 1 else FLAST
                dve.wait_ge(h_hid, j + 1)
                dve.tensor_tensor(h_lo[0:rows, f, :], hid[0:rows, j % 2, :], h_hi[0:rows, f, :],
                                  ALU.subtract).then_inc(h_lod, 1)

            xn_low(TT - 2, ps_t[:, 0, :])
            add_last(2)
            xn_low(TT - 1, ps_t[:, 1, :])
            add_last(3)
            dve.wait_ge(sc_cv, 4)

            def finish(t):
                i = t % TT
                q = newest()
                link(dve.tensor_scalar(z[:, i, :], z[:, i, :], mv[:, q, 0:1], rstd[:, q:q + 1],
                                       ALU.subtract, ALU.mult))
                zi = z[:, i, :].rearrange("p (k c) -> p k c", k=KT)
                dve.tensor_tensor(zi, zi, rows_of(t), ALU.add).then_inc(out_rdy, 1)

            for c in range(NB):
                for f in range(FT):
                    j = c * FT + f
                    rows = P if f < FT - 1 else FLAST
                    if c + 1 < NB and f in (4, 6, 8, 10):
                        xn_low((c + 1) * TT + (f - 4) // 2, ps_t[:, 1, :])
                    dve.wait_ge(silu_done, j + 1)
                    dve.wait_ge(u_ps, j + 1)
                    after(dve, h_lod, j - 1)
                    dve.scalar_tensor_tensor(hid[0:rows, j % 2, :], gu_bank[2 * (j % 2) + 1][0:rows, :],
                                             up_f[0:rows, f:f + 1], silu[0:rows, j % 2, :],
                                             ALU.mult, ALU.mult).then_inc(hid_done, 1)
                    if f:
                        hidden_low(c, f - 1)
                    if c + 1 < NB:
                        t = (c + 1) * TT + f // 2
                        if f in (2, 4, 6, 8):
                            to_xn(t - 1)
                        if f in (0, 2, 4, 6):
                            rows_first(t)
                        if f in (1, 3, 5, 7):
                            rows_add(t)
                hidden_low(c, FT - 1)
                for i in range(TT):
                    t = c * TT + i
                    dve.wait_ge(d_ps, t + 1)
                    after(dve, out_dma[i], 16 * c)
                    dve.tensor_tensor(z[:, i, :], ps_p[:, t % 2, :], down_f[:, :], ALU.mult).then_inc(z_done, 1)
                    dve.wait_ge(z_done, t + 1)
                    statistics(z[:, i, :])
                    finish(t)


def rope_tables():
    import numpy as np
    f32 = np.float32
    inv = f32(1.0) / f32(10000.0) ** (np.arange(0, HD, 2, dtype=f32) / f32(HD))
    angle = np.arange(S, dtype=f32)[:, None] * inv[None, :]
    up = f32(QK_UP / (X_UP * W_UP))
    cos, sin = np.cos(angle).T * up, np.sin(angle).T * up
    return np.concatenate([cos, cos]).astype(f32), np.concatenate([-sin, sin]).astype(f32)


def halves(a):
    import numpy as np
    r, c = a.shape
    return np.ascontiguousarray(a.reshape(r, c // HD, HD // 2, 2).transpose(0, 1, 3, 2).reshape(r, c))


def by_group(*arrays):
    import numpy as np
    return np.concatenate([a.reshape(a.shape[0], NKV, -1).transpose(1, 0, 2) for a in arrays], axis=2)


def by_partition(scales):
    import numpy as np
    return np.pad(scales, (0, FT * P - DFF)).reshape(FT, P).T


def kernel(**inputs):
    import numpy as np
    import concourse.bacc as bacc
    from concourse.bass_utils import run_bass_kernel_spmd

    given = {k.replace("L0_", "").replace("attn_", "").replace("ffn_", ""): np.asarray(v) for k, v in inputs.items()}
    cos, sin = rope_tables()
    arrays = {
        "x": given["hidden_states"],
        "w_codes": by_group(halves(given["q_codes"]), halves(given["k_codes"]), given["v_codes"]),
        "w_scales": by_group(halves(given["q_scales"]), halves(given["k_scales"]), given["v_scales"]),
        "o_codes": given["o_codes"],
        "o_scales": given["o_scales"].reshape(NH, KT, P).transpose(2, 0, 1),
        "gate_t": given["gate_w"].T, "gate_s": by_partition(given["gate_s"]),
        "up_t": given["up_w"].T, "up_s": by_partition(given["up_s"]),
        "down_t": given["down_w"].T, "down_s": given["down_s"],
        "cos_t": cos, "sin_t": sin,
        "ident_in": np.eye(P, dtype=np.float32), "mask_in": np.triu(np.ones((P, P), np.float32), 1),
    }
    arrays = {k: np.ascontiguousarray(v) for k, v in arrays.items()}
    nc = bacc.Bacc("TRN2", target_bir_lowering=False, num_devices=1)
    args = [nc.dram_tensor(k, v.shape, mybir.dt.from_np(v.dtype), kind="ExternalInput").ap() for k, v in arrays.items()]
    out = nc.dram_tensor("out", (NB, S, D), F32, kind="ExternalOutput").ap()
    layer(nc, *args, out)
    return run_bass_kernel_spmd(nc, [arrays], core_ids=[0]).results[0]["out"]
```
